# Optimizing a Trainium2 kernel written in Bass

```python
import numpy as np
import jax
import jax.numpy as jnp

def _softmax(x, axis=-1):
    return jax.nn.softmax(x, axis=axis)

def _gelu(x):
    return jax.nn.gelu(x, approximate=True)

def _silu(x):
    return jax.nn.silu(x)

def _sigmoid(x):
    return jax.nn.sigmoid(x)

def _layernorm(x, axis=-1, eps=1e-05):
    m = jnp.mean(x, axis=axis, keepdims=True)
    v = jnp.var(x, axis=axis, keepdims=True)
    return (x - m) / jnp.sqrt(v + eps)

def _scatter_add(tgt, idx, src, axis=0):
    return tgt.at[idx].add(src)

def _segment_sum(src, seg, n):
    return jax.ops.segment_sum(src, seg, n)
kernel_name = 'mk_xattn_ffn_d2_seqx_r4_57630e'

def setup_inputs(seed: int=0):
    np.random.seed(seed)
    _w = jnp.asarray

    def _rec_inputs():
        import jax
        import jax.numpy as jnp
        _rk = jax.random.key(seed)
        x = -0.0002928 + 1 * jax.random.normal(jax.random.fold_in(_rk, 1), (4, 512, 256), jnp.float32)
        _lenS = 512 - jax.random.randint(jax.random.fold_in(_rk, 7), (4,), 0, max(1, 512 // 4) + 1, jnp.int32)
        _lenS2 = 512 - jax.random.randint(jax.random.fold_in(_rk, 8), (4,), 0, max(1, 512 // 4) + 1, jnp.int32)
        _ctx_1024P = jax.random.normal(jax.random.fold_in(_rk, 11), (4, 16, 256), jnp.float32)
        _ctx_1024c = jax.random.dirichlet(jax.random.fold_in(_rk, 511), 0.3 * jnp.ones((16,), jnp.float32), (4, 512))
        _ctx_1024t = jnp.einsum('bsk,bkd->bsd', _ctx_1024c, _ctx_1024P)
        _ctx_1024t = _ctx_1024t * jax.lax.rsqrt(jnp.mean(jnp.square(_ctx_1024t)) + 1e-12) * 0.953939
        ctx_1024 = -1.39393e-06 + 0.999914 * (_ctx_1024t + 0.3 * jax.random.normal(jax.random.fold_in(_rk, 611), (4, 512, 256), jnp.float32))
        return (x, ctx_1024)
    x, ctx_1024 = _rec_inputs()

    def _L0_xattn_setup():
        import jax, jax.numpy as jnp
        import numpy as np
        ROPE_BASE = 10000.0

        def rotate_half(x):
            d = x.shape[-1] // 2
            return jnp.concatenate([-x[..., d:], x[..., :d]], axis=-1)

        def rope_cos_sin(seq_len, head_dim, dtype=jnp.float32):
            inv_freq = 1.0 / ROPE_BASE ** (jnp.arange(0, head_dim, 2, dtype=jnp.float32) / head_dim)
            t = jnp.arange(seq_len, dtype=jnp.float32)
            freqs = jnp.outer(t, inv_freq)
            emb = jnp.concatenate([freqs, freqs], axis=-1)
            return (jnp.cos(emb).astype(dtype), jnp.sin(emb).astype(dtype))

        def alibi_slopes(num_heads):
            return jnp.asarray([2.0 ** (-8.0 * i / num_heads) for i in range(1, num_heads + 1)], dtype=jnp.float32)
        key = jax.random.key(seed)
        k1, k2, k3 = jax.random.split(key, 3)
        B, T, H = (2, 512, 256)
        return {'q': jax.random.normal(k1, (B, T, H), dtype=jnp.float32), 'k': jax.random.normal(k2, (B, T, H), dtype=jnp.float32), 'v': jax.random.normal(k3, (B, T, H), dtype=jnp.float32), 'num_heads': 16}
    _L0_xattn_all = _L0_xattn_setup()
    _L0_xattn_in = {k: v for k, v in _L0_xattn_all.items() if k in ()}
    del _L0_xattn_all

    def _L0_ffn_setup():
        import jax, jax.numpy as jnp
        import numpy as np
        B, T, D, F, E = (2, 256, 256, 1024, 8)
        EPS = 1e-06
        key = jax.random.key(seed)
        k = jax.random.split(key, 5)
        scale = 0.02
        return {'x': jax.random.normal(k[0], (B, T, D), dtype=jnp.float32), 'rms_w': jnp.ones((D,), dtype=jnp.float32), 'gate_w': jax.random.normal(k[1], (E, D), dtype=jnp.float32) * scale, 'W1': jax.random.normal(k[2], (E, D, F), dtype=jnp.float32) * scale, 'b1': jnp.zeros((E, F), dtype=jnp.float32), 'W2': jax.random.normal(k[3], (E, F, D), dtype=jnp.float32) * scale, 'b2': jnp.zeros((E, D), dtype=jnp.float32)}
    _L0_ffn_all = _L0_ffn_setup()
    _L0_ffn_in = {k: v for k, v in _L0_ffn_all.items() if k in ('rms_w', 'gate_w', 'W1', 'b1', 'W2', 'b2')}
    del _L0_ffn_all

    def _L1_xattn_setup():
        import jax, jax.numpy as jnp
        import numpy as np
        HIDDEN = 256
        HEADS = 16
        D_K = HIDDEN // HEADS
        B, S = (2, 512)
        key = jax.random.key(seed)
        ks = jax.random.split(key, 11)
        sc = 1.0 / np.sqrt(HIDDEN)
        inp = {'q': jax.random.normal(ks[0], (B, S, HIDDEN), jnp.float32), 'k': jax.random.normal(ks[1], (B, S, HIDDEN), jnp.float32), 'v': jax.random.normal(ks[2], (B, S, HIDDEN), jnp.float32), 'Wq': jax.random.normal(ks[3], (HIDDEN, HIDDEN), jnp.float32) * sc, 'bq': jnp.zeros((HIDDEN,), jnp.float32), 'Wk': jax.random.normal(ks[4], (HIDDEN, HIDDEN), jnp.float32) * sc, 'bk': jnp.zeros((HIDDEN,), jnp.float32), 'Wv': jax.random.normal(ks[5], (HIDDEN, HIDDEN), jnp.float32) * sc, 'bv': jnp.zeros((HIDDEN,), jnp.float32), 'Wo': jax.random.normal(ks[6], (HIDDEN, HIDDEN), jnp.float32) * sc, 'bo': jnp.zeros((HIDDEN,), jnp.float32)}
        return inp
    _L1_xattn_all = _L1_xattn_setup()
    _L1_xattn_in = {k: v for k, v in _L1_xattn_all.items() if k in ('Wq', 'bq', 'Wk', 'bk', 'Wv', 'bv', 'Wo', 'bo')}
    del _L1_xattn_all

    def _L1_ffn_setup():
        import jax, jax.numpy as jnp
        import numpy as np
        N, T, D = (4, 1024, 256)
        NUM_EXPERTS = 8
        EXPERT_CAP = 2.0
        MLP_RATIO = 4
        HIDDEN = MLP_RATIO * D
        key = jax.random.key(seed)
        k1, k2, k3, k4 = jax.random.split(key, 4)
        x = jax.random.normal(k1, (N, T, D), dtype=jnp.float32)
        gate_w = jax.random.truncated_normal(k2, -2.0, 2.0, (D, NUM_EXPERTS), dtype=jnp.float32) * 0.02
        w1 = jax.random.normal(k3, (NUM_EXPERTS, D, HIDDEN), dtype=jnp.float32) * 0.02
        w2 = jax.random.normal(k4, (NUM_EXPERTS, HIDDEN, D), dtype=jnp.float32) * 0.02
        return {'x': x, 'gate_w': gate_w, 'w1': w1, 'w2': w2}
    _L1_ffn_all = _L1_ffn_setup()
    _L1_ffn_in = {k: v for k, v in _L1_ffn_all.items() if k in ('gate_w', 'w1', 'w2')}
    del _L1_ffn_all
    return {'x': x, 'ctx_1024': ctx_1024, 'L0_ffn_rms_w': _L0_ffn_in['rms_w'], 'L0_ffn_gate_w': _L0_ffn_in['gate_w'], 'L0_ffn_W1': _L0_ffn_in['W1'], 'L0_ffn_b1': _L0_ffn_in['b1'], 'L0_ffn_W2': _L0_ffn_in['W2'], 'L0_ffn_b2': _L0_ffn_in['b2'], 'L1_xattn_Wq': _L1_xattn_in['Wq'], 'L1_xattn_bq': _L1_xattn_in['bq'], 'L1_xattn_Wk': _L1_xattn_in['Wk'], 'L1_xattn_bk': _L1_xattn_in['bk'], 'L1_xattn_Wv': _L1_xattn_in['Wv'], 'L1_xattn_bv': _L1_xattn_in['bv'], 'L1_xattn_Wo': _L1_xattn_in['Wo'], 'L1_xattn_bo': _L1_xattn_in['bo'], 'L1_ffn_gate_w': _L1_ffn_in['gate_w'], 'L1_ffn_w1': _L1_ffn_in['w1'], 'L1_ffn_w2': _L1_ffn_in['w2']}

def reference(x, ctx_1024, L0_ffn_rms_w, L0_ffn_gate_w, L0_ffn_W1, L0_ffn_b1, L0_ffn_W2, L0_ffn_b2, L1_xattn_Wq, L1_xattn_bq, L1_xattn_Wk, L1_xattn_bk, L1_xattn_Wv, L1_xattn_bv, L1_xattn_Wo, L1_xattn_bo, L1_ffn_gate_w, L1_ffn_w1, L1_ffn_w2):
    import jax
    import jax.numpy as jnp

    def _L0_xattn_ref(q, k, v, num_heads):
        import jax, jax.numpy as jnp
        import numpy as np
        ROPE_BASE = 10000.0

        def rotate_half(x):
            d = x.shape[-1] // 2
            return jnp.concatenate([-x[..., d:], x[..., :d]], axis=-1)

        def rope_cos_sin(seq_len, head_dim, dtype=jnp.float32):
            inv_freq = 1.0 / ROPE_BASE ** (jnp.arange(0, head_dim, 2, dtype=jnp.float32) / head_dim)
            t = jnp.arange(seq_len, dtype=jnp.float32)
            freqs = jnp.outer(t, inv_freq)
            emb = jnp.concatenate([freqs, freqs], axis=-1)
            return (jnp.cos(emb).astype(dtype), jnp.sin(emb).astype(dtype))

        def alibi_slopes(num_heads):
            return jnp.asarray([2.0 ** (-8.0 * i / num_heads) for i in range(1, num_heads + 1)], dtype=jnp.float32)
        B, T, H = q.shape
        nh = num_heads
        hd = H // nh
        q = q.reshape(B, T, nh, hd)
        k = k.reshape(B, T, nh, hd)
        v = v.reshape(B, T, nh, hd)
        cos, sin = rope_cos_sin(T, hd, q.dtype)
        cos = cos[None, :, None, :]
        sin = sin[None, :, None, :]
        q = q * cos + rotate_half(q) * sin
        k = k * cos + rotate_half(k) * sin
        rel = jnp.arange(T)[None, :] - jnp.arange(T)[:, None]
        bias = alibi_slopes(nh)[:, None, None] * rel.astype(q.dtype)
        scale = 1.0 / jnp.sqrt(jnp.asarray(hd, dtype=q.dtype))
        scores = jnp.einsum('bqhd,bkhd->bhqk', q, k) * scale + bias[None]
        attn = jax.nn.softmax(scores, axis=-1)
        out = jnp.einsum('bhqk,bkhd->bqhd', attn, v)
        return out.reshape(B, T, H)

    def _L0_ffn_ref(x, rms_w, gate_w, W1, b1, W2, b2):
        import jax, jax.numpy as jnp
        import numpy as np
        B, T, D, F, E = (2, 256, 256, 1024, 8)
        EPS = 1e-06
        ms = jnp.mean(x * x, axis=-1, keepdims=True)
        xn = x * jax.lax.rsqrt(ms + EPS) * rms_w
        logits = jnp.einsum('btd,ed->bte', xn, gate_w)
        scores = jax.nn.softmax(logits, axis=-1)
        top1_idx = jnp.argmax(scores, axis=-1)
        top1_score = jnp.max(scores, axis=-1)
        out = jnp.zeros_like(xn)
        for e in range(E):
            h = jax.nn.silu(jnp.einsum('btd,df->btf', xn, W1[e]) + b1[e])
            ye = jnp.einsum('btf,fd->btd', h, W2[e]) + b2[e]
            out = jnp.where((top1_idx == e)[..., None], ye, out)
        return out * top1_score[..., None]

    def _L1_xattn_ref(q, k, v, Wq, bq, Wk, bk, Wv, bv, Wo, bo):
        import jax, jax.numpy as jnp
        import numpy as np
        HIDDEN = 256
        HEADS = 16
        D_K = HIDDEN // HEADS
        B, S = (2, 512)
        bs = q.shape[0]

        def proj(x, W, b):
            y = x @ W.T + b
            return y.reshape(bs, -1, HEADS, D_K).transpose(0, 2, 1, 3)
        qh, kh, vh = (proj(q, Wq, bq), proj(k, Wk, bk), proj(v, Wv, bv))
        scores = jnp.einsum('bhqd,bhkd->bhqk', qh, kh) / jnp.sqrt(jnp.float32(D_K))
        attn = jax.nn.softmax(scores, axis=-1)
        x = jnp.einsum('bhqk,bhkd->bhqd', attn, vh)
        x = x.transpose(0, 2, 1, 3).reshape(bs, -1, HEADS * D_K)
        return x @ Wo.T + bo

    def _L1_ffn_ref(x, gate_w, w1, w2):
        import jax, jax.numpy as jnp
        import numpy as np
        N, T, D = (4, 1024, 256)
        NUM_EXPERTS = 8
        EXPERT_CAP = 2.0
        MLP_RATIO = 4
        HIDDEN = MLP_RATIO * D
        x = x.astype(jnp.float32)
        n, t, d = x.shape
        k = int(EXPERT_CAP * t / NUM_EXPERTS)
        scores = jnp.einsum('ntd,de->nte', x, gate_w)
        probs = jax.nn.softmax(scores, axis=-1)
        probs = jnp.transpose(probs, (0, 2, 1))
        g, m = jax.lax.top_k(probs, k)
        xin = jax.vmap(lambda xb, mb: xb[mb])(x, m)
        h = jax.nn.gelu(jnp.einsum('nekd,edf->nekf', xin, w1))
        h = jnp.einsum('nekf,efd->nekd', h, w2)
        weighted = g[..., None] * h
        flat_idx = (m + jnp.arange(n, dtype=m.dtype)[:, None, None] * t).reshape(-1)
        out = jnp.zeros((n * t, d), dtype=jnp.float32).at[flat_idx].add(weighted.reshape(-1, d))
        out = out.reshape(n, t, d)
        return out.astype(jnp.bfloat16)
    x = x + _L0_xattn_ref(_layernorm(x, axis=-1), ctx_1024, ctx_1024, 16)
    x = x + _L0_ffn_ref(_layernorm(x, axis=-1), L0_ffn_rms_w, L0_ffn_gate_w, L0_ffn_W1, L0_ffn_b1, L0_ffn_W2, L0_ffn_b2)
    x = x + _L1_xattn_ref(_layernorm(x, axis=-1), ctx_1024, ctx_1024, L1_xattn_Wq, L1_xattn_bq, L1_xattn_Wk, L1_xattn_bk, L1_xattn_Wv, L1_xattn_bv, L1_xattn_Wo, L1_xattn_bo)
    x = x + _L1_ffn_ref(_layernorm(x, axis=-1), L1_ffn_gate_w, L1_ffn_w1, L1_ffn_w2)
    return x

_drawn_inputs = setup_inputs


def setup_inputs(seed=0):
    import zlib

    import numpy as np

    out = dict(_drawn_inputs(seed))
    spreads = {'L0_ffn_rms_w': (1.0, 0.6),
     'L0_ffn_b1': (0.0, 0.8),
     'L0_ffn_b2': (0.0, 0.509),
     'L1_xattn_bq': (0.0, 0.514),
     'L1_xattn_bk': (0.0, 0.8),
     'L1_xattn_bv': (0.0, 0.1),
     'L1_xattn_bo': (0.0, 0.1)}
    factors = {'L0_ffn_W1': 3.303,
     'L0_ffn_W2': 3.098,
     'L1_ffn_gate_w': 3.48,
     'L1_ffn_w1': 3.086,
     'L1_ffn_w2': 3.009}
    for name, (base, spread) in spreads.items():
        noise = np.random.default_rng([zlib.crc32(name.encode()), seed]).standard_normal(out[name].shape)
        drawn = base * np.exp(spread * noise) if base else spread * noise
        out[name] = jnp.asarray(drawn.astype(out[name].dtype))
    for name, factor in factors.items():
        out[name] = (out[name] * factor).astype(out[name].dtype)
    return out
```

```python
from contextlib import ExitStack

import concourse.bass as bass
from concourse import mybir

ALU = mybir.AluOpType
ACT = mybir.ActivationFunctionType
AX = mybir.AxisListType
F32 = mybir.dt.float32
F32R = mybir.dt.float32r
BF16 = mybir.dt.bfloat16
I32 = mybir.dt.int32
U32 = mybir.dt.uint32

P = 128
B, T, D = 4, 512, 256
H, HD = 16, 16
E, F = 8, 1024
NT = B * T // P
TB = T // P
DC = D // P
FC = F // P
HG = 4
NG = H // HG
SLOTS = B * NG
STEPS = SLOTS * TB
VW = 32
BIAS_ROW = 3 * HD
MAX_ROW = 96
MAX_ROWS = 2 * HG
K_ROWS = MAX_ROW + MAX_ROWS
SEL_TILES = B * T // P + E
CAP = 2 * T // E
LN_EPS = 1e-5
RMS_EPS = 1e-6
RSQRT_MAGIC = float(0x5F3759DF)
W0_COLS = DC * F + FC * D + FC + D


class Counter:

    def __init__(self, eng, sem):
        self.eng, self.sem, self.n = eng, sem, 0

    def link(self, ins):
        self.n += 1
        ins.then_inc(self.sem, 1)
        self.eng.wait_ge(self.sem, self.n)


def wait_from(eng, sem, value):
    if not isinstance(value, int) or value > 0:
        eng.wait_ge(sem, value)


def turns(eng, n, body):
    body(0)
    with eng.Fori(1, n) as it:
        body(it)


def rsqrt(dve, chain, y, x, tmp, scale, eps):
    v, u = tmp
    chain.link(dve.tensor_scalar(v, x, scale, eps, ALU.mult, ALU.add))
    chain.link(dve.tensor_scalar(u.bitcast(I32), v.bitcast(I32), 1, None, ALU.logical_shift_right))
    chain.link(dve.tensor_scalar(y.bitcast(I32), u.bitcast(I32), -1.0, RSQRT_MAGIC, ALU.mult, ALU.add))
    for _ in range(4):
        chain.link(dve.tensor_tensor(u, y, y, ALU.mult))
        chain.link(dve.scalar_tensor_tensor(u, u, -0.5, v, ALU.mult, ALU.mult))
        chain.link(dve.scalar_tensor_tensor(y, u, 1.5, y, ALU.add, ALU.mult))


class Memory:
    pass


def attention_schedule(layer):
    jobs = {t: [] for t in range(-9, STEPS + 6)}
    qkinds = ["q"] if layer == 0 else ["qt", "q"]
    if layer == 1:
        jobs[-9] += [("k", 0, 0), ("k", 0, 1), ("v", 0, 0), ("v", 0, 1)]
    jobs[-9] += [(kind, i) for i in range(TB) for kind in qkinds]
    for s in range(SLOTS):
        jobs[4 * s - 4].append(("m", s))
        jobs[4 * s + 5].append(("o", s))
    for b in range(1, B):
        for j, dt in enumerate((-18, -17, -14, -13)):
            t = max(16 * b + dt, -8)
            jobs[t] += [(kind, TB * b + j) for kind in qkinds]
        if layer == 1:
            jobs[16 * b - 20].append(("k", b, 0))
            jobs[16 * b - 19].append(("k", b, 1))
            jobs[16 * b - 12].append(("v", b, 0))
            jobs[16 * b - 11].append(("v", b, 1))
    if layer == 1:
        for b in range(B):
            t = 16 * b + 18
            jobs[t] += [("at", b, 0), ("at", b, 1)]
            jobs[t + 1] += [("a", b, 0), ("a", b, 1)]
    index, n = {}, 0
    for t in sorted(jobs):
        for job in jobs[t]:
            index[job] = n
            n += 1
    return jobs, index


def attention(nc, m, layer, dram):
    jobs, index = attention_schedule(layer)
    LT = sorted(jobs)
    with ExitStack() as ctx:
        def sb(name, shape, dt):
            return ctx.enter_context(nc.sbuf_tensor(f"a{layer}_{name}", shape, dt))

        def sem(name):
            return m.ctx.enter_context(nc.semaphore(f"a{layer}_{name}"))

        ka = sb("ka", [P, NG, HG, T], F32R)
        qa = sb("qa", [P, NG, HG, T], F32R)
        probs = sb("probs", [P, 3, HG, T], F32)
        vaug = sb("vaug", [P, 2, TB, H, VW], F32)
        ctx_t = sb("ctx_t", [P, 2, DC, T], F32)
        kf = sb("kf", [P, DC, T], F32)
        kst = sb("kst", [P, 2, DC, T], F32R)
        qst = sb("qst", [P, 2, 2, DC, P], F32R)
        xn = sb("xn", [P, 2, D], F32)
        neg_max = sb("neg_max", [P, 2, TB, 2, HG], F32R)
        row_max = sb("row_max", [P, 3, HG, TB], F32)
        max_t = sb("max_t", [MAX_ROWS, 2, T], F32R)
        out_sb = sb("out_sb", [P, T], F32)
        rden = sb("rden", [P, TB, HG], F32)
        stats = sb("stats", [P, TB, 6], F32)
        mv = sb("mv", [P, NT, 2], F32)
        rstd = sb("rstd", [P, NT], F32)
        tmp = [sb(f"tmp{i}", [P, TB], F32) for i in range(2)]
        if layer == 0:
            ctx_r = sb("ctx_r", [P, 2, DC, T], F32)
            ctx_v = sb("ctx_v", [P, 2, TB, D], F32)
            kf2 = sb("kf2", [P, DC, T], F32)
            cos_t = sb("cos_t", [P, T], F32)
            sin_t = sb("sin_t", [P, T], F32)
            cos_q = sb("cos_q", [P, TB, HD], F32)
            sin_q = sb("sin_q", [P, TB, HD], F32)
            rope_a = sb("rope_a", [P, D], F32)
            rope_b = sb("rope_b", [P, D], F32)
            att = sb("att", [P, 2, TB, HG * HD], F32)
        else:
            wq, wk, wv, wo = (sb(f"w{c}", [P, DC, D], F32) for c in "qkvo")
            bqk = sb("bqk", [P, 2, DC], F32)
            bv = sb("bv", [P, D], F32)
            bo = sb("bo", [P, D], F32)
            xnt = sb("xnt", [P, 2, DC, P], F32)
            qf = sb("qf", [P, 2, DC, P], F32)
            att = sb("att", [P, 2, TB, D], F32)
            att_t = sb("att_t", [P, DC, T], F32)

        x_in = [sem(f"x_in{b}") for b in range(B)]
        consts_in = sem("consts_in")
        rows_in = sem("rows_in")
        vaug_set = sem("vaug_set")
        ctx_in = [sem(f"ctx_in{i}") for i in range(2)]
        ctx_used = sem("ctx_used")
        k_ready = sem("k_ready")
        k_stored = sem("k_stored")
        q_ready = sem("q_ready")
        q_stored = [sem(f"q_stored{i}") for i in range(2)]
        loaded = [sem(f"loaded{i}") for i in range(NG)]
        stats_done = sem("stats_done")
        xn_ready = sem("xn_ready")
        misc_full = sem("misc_full")
        misc_free = sem("misc_free")
        mx_full = sem("mx_full")
        mx_read = sem("mx_read")
        neg_ready = sem("neg_ready")
        max_in = [sem(f"max_in{i}") for i in range(NG)]
        st_full = sem("st_full")
        exp_done = sem("exp_done")
        v_ready = sem("v_ready")
        pv_done = sem("pv_done")
        out_copied = sem("out_copied")
        att_added = sem("att_added")
        dve_chain = sem("dve_chain")
        pool_chain = sem("pool_chain")

        x = m.x
        misc = m.ps_misc
        n_const = 4 if layer == 0 else 7
        n_ctx = 3 if layer == 0 else 1
        k_scr = dram["k_scr"]
        q_scr = dram["q_scr"]

        with nc.Block() as block:

            @block.sync
            def _(sp):
                def load_ctx(b):
                    if b >= B:
                        return
                    if b >= 2:
                        sp.wait_ge(ctx_used, b - 1)
                    sp.dma_start(ctx_t[:, b % 2], dram["ctx_t"][b].rearrange("(c p) t -> p c t", p=P)).then_inc(ctx_in[b % 2], 16)
                    if layer == 0:
                        sp.dma_start(ctx_r[:, b % 2], dram["ctx_r"][b].rearrange("(c p) t -> p c t", p=P)).then_inc(ctx_in[b % 2], 16)
                        sp.dma_start(ctx_v[:, b % 2], dram["ctx"][b].rearrange("(j p) d -> p j d", p=P)).then_inc(ctx_in[b % 2], 16)

                def store_k(b):
                    sp.wait_ge(k_ready, b + 1)
                    for part in range(2):
                        sp.dma_start(k_scr[b, part].rearrange("(c p) t -> p c t", p=P), kst[:, part].bitcast(F32)).then_inc(k_stored, 16)

                def store_q(i):
                    b, j = i // TB, i % TB
                    sp.wait_ge(q_ready, i + 1)
                    for part in range(2):
                        sp.dma_start(q_scr[b, part, :, j * P:(j + 1) * P].rearrange("(c p) t -> p c t", p=P),
                                     qst[:, i % 2, part].bitcast(F32)).then_inc(q_stored[i % 2], 16)

                def load_group(b, g):
                    s = NG * b + g
                    if g == 0:
                        sp.wait_ge(k_stored, 32 * (b + 1))
                        for i in range(2):
                            sp.wait_ge(q_stored[i], 32 * (TB // 2) * (b + 1))
                    if b >= 1:
                        sp.wait_ge(st_full, 8 * (s - NG + 1))
                    rows = slice(g * HG * HD, (g + 1) * HG * HD)
                    for r, (qpart, kpart) in enumerate(((0, 0), (1, 0), (0, 1))):
                        sp.dma_start(qa[HD * r:HD * (r + 1), g].bitcast(F32), q_scr[b, qpart, rows].rearrange("(h d) t -> d h t", d=HD)).then_inc(loaded[g], 16)
                        sp.dma_start(ka[HD * r:HD * (r + 1), g].bitcast(F32), k_scr[b, kpart, rows].rearrange("(h d) t -> d h t", d=HD)).then_inc(loaded[g], 16)

                load_ctx(0)
                if layer == 0:
                    sp.dma_start(x[:, 0:TB], dram["x"][0].rearrange("(j p) d -> p j d", p=P)).then_inc(x_in[0], 16)
                    for dst, src in ((cos_t, "cos_t"), (sin_t, "sin_t"), (cos_q, "cos_q"), (sin_q, "sin_q")):
                        sp.dma_start(dst[:], dram[src]).then_inc(consts_in, 16)
                    sp.dma_start(m.ident[:], dram["ident"]).then_inc(m.ident_in, 16)
                    for b in range(1, B):
                        sp.dma_start(x[:, TB * b:TB * (b + 1)], dram["x"][b].rearrange("(j p) d -> p j d", p=P)).then_inc(x_in[b], 16)
                else:
                    for dst, src in ((wq, "wq"), (wk, "wk"), (wv, "wv"), (wo, "wo"), (bqk, "bqk"), (bv, "bv"), (bo, "bo")):
                        sp.dma_start(dst[:], dram[src]).then_inc(consts_in, 16)
                load_ctx(1)
                store_k(0)
                for i in range(TB):
                    store_q(i)
                for g in range(NG):
                    load_group(0, g)
                load_ctx(2)
                for t in LT[1:]:
                    for b in range(1, B):
                        if t == 16 * b - 18:
                            store_k(b)
                        if t == 16 * b - 12:
                            load_ctx(b + 2)
                    for job in jobs[t]:
                        if job[0] == "q":
                            store_q(job[1])
                    for b in range(1, B):
                        for g in range(NG):
                            if t == 16 * b - 12 + 4 * g:
                                load_group(b, g)

            @block.gpsimd
            def _(pool):
                chain = Counter(pool, pool_chain)
                if layer == 0:
                    for g in range(NG):
                        pool.dma_start(ka[BIAS_ROW:K_ROWS, g], dram["k_rows"][g]).then_inc(rows_in, 16)
                        pool.dma_start(qa[BIAS_ROW:MAX_ROW, g], dram["q_rows"][g]).then_inc(rows_in, 16)
                else:
                    for g in range(NG):
                        pool.dma_start(ka[BIAS_ROW:K_ROWS, g], dram["k_rows"][NG + g]).then_inc(rows_in, 16)
                        pool.dma_start(qa[BIAS_ROW:MAX_ROW, g], dram["q_rows"][g]).then_inc(rows_in, 16)

                def keys(b):
                    if layer == 0:
                        if b == 0:
                            pool.wait_ge(consts_in, 16 * n_const)
                        pool.wait_ge(ctx_in[b % 2], 16 * n_ctx * (b // 2 + 1))
                        pool.tensor_tensor(kf[:], ctx_t[:, b % 2], cos_t[:].unsqueeze(1).to_broadcast([P, DC, T]), ALU.mult)
                        chain.link(pool.tensor_tensor(kf2[:], ctx_r[:, b % 2], sin_t[:].unsqueeze(1).to_broadcast([P, DC, T]), ALU.mult))
                        chain.link(pool.tensor_tensor(kf[:], kf[:], kf2[:], ALU.add))
                    else:
                        pool.wait_ge(misc_free, index["k", b, 1] + 1)
                    if b >= 1:
                        pool.wait_ge(k_stored, 32 * b)
                    chain.link(pool.tensor_copy(kst[:, 0], kf[:]))
                    pool.tensor_tensor(kst[:, 1], kf[:], kst[:, 0].bitcast(F32), ALU.subtract).then_inc(k_ready, 1)

                def values(b):
                    if b >= 2:
                        pool.wait_ge(pv_done, 16 * (b - 1))
                    pool.wait_ge(vaug_set, 2)
                    pool.tensor_copy(vaug[:, b % 2, :, :, 0:HD], ctx_v[:, b % 2].rearrange("p j (h d) -> p j h d", d=HD)).then_inc(v_ready, 1)
                    pool.wait_ge(v_ready, b + 1)
                    pool.engine_nop().then_inc(ctx_used, 1)

                def normed(i):
                    b, j = i // TB, i % TB
                    pool.wait_ge(stats_done, b + 1)
                    if i >= 2:
                        pool.wait_ge(misc_full, index["q" if layer == 0 else "qt", i - 2] + 1)
                    if layer == 1:
                        pool.tensor_scalar(xn[:, i % 2], x[:, i], mv[:, i, 0:1], rstd[:, i:i + 1], ALU.subtract, ALU.mult).then_inc(xn_ready, 1)
                        return
                    chain.link(pool.tensor_scalar(xn[:, i % 2], x[:, i], mv[:, i, 0:1], rstd[:, i:i + 1], ALU.subtract, ALU.mult))
                    xh = xn[:, i % 2].rearrange("p (h d) -> p h d", d=HD)
                    ah = rope_a[:].rearrange("p (h d) -> p h d", d=HD)
                    bh = rope_b[:].rearrange("p (h d) -> p h d", d=HD)
                    cb = cos_q[:, j].unsqueeze(1).to_broadcast([P, H, HD])
                    half = HD // 2
                    pool.tensor_tensor(ah, xh, cb, ALU.mult)
                    pool.tensor_tensor(bh[:, :, 0:half], xh[:, :, half:HD], sin_q[:, j, 0:half].unsqueeze(1).to_broadcast([P, H, half]), ALU.mult)
                    chain.link(pool.tensor_tensor(bh[:, :, half:HD], xh[:, :, 0:half], sin_q[:, j, half:HD].unsqueeze(1).to_broadcast([P, H, half]), ALU.mult))
                    pool.tensor_tensor(xn[:, i % 2], rope_a[:], rope_b[:], ALU.add).then_inc(xn_ready, 1)

                def split_q(i):
                    pool.wait_ge(misc_free, index["q", i] + 1)
                    if i >= 2:
                        pool.wait_ge(q_stored[i % 2], 32 * (i // 2))
                    chain.link(pool.tensor_copy(qst[:, i % 2, 0], qf[:, i % 2]))
                    pool.tensor_tensor(qst[:, i % 2, 1], qf[:, i % 2], qst[:, i % 2, 0].bitcast(F32), ALU.subtract).then_inc(q_ready, 1)

                if layer == 0:
                    keys(0)
                    values(0)
                    for i in range(TB):
                        normed(i)
                else:
                    normed(0)
                    keys(0)
                    for i in range(TB):
                        if i:
                            normed(i)
                        if i:
                            split_q(i - 1)
                    split_q(TB - 1)
                for t in LT[1:]:
                    for b in range(1, B):
                        if t == 16 * b - 19:
                            keys(b)
                        if layer == 0 and t == 16 * b - 12:
                            values(b)
                    for job in jobs[t + 1] if t + 1 in jobs else []:
                        if job[0] == ("q" if layer == 0 else "qt"):
                            normed(job[1])
                    for job in jobs[t]:
                        if job[0] == "q" and layer == 1:
                            split_q(job[1])
                        if job[0] == "o" and layer == 0:
                            s = job[1]
                            b, g = s // NG, s % NG
                            pool.wait_ge(misc_free, index[job] + 1)
                            xs = x[:, TB * b:TB * (b + 1), g * HG * HD:(g + 1) * HG * HD]
                            pool.tensor_tensor(xs, xs, att[:, s % 2], ALU.add).then_inc(att_added, 1)
                        if job[0] == "a" and job[2] == 1:
                            b = job[1]
                            pool.wait_ge(misc_free, index[job] + 1)
                            xs = x[:, TB * b:TB * (b + 1)]
                            pool.tensor_tensor(xs, xs, bo[:].unsqueeze(1).to_broadcast([P, TB, D]), ALU.add).then_inc(att_added, 1)

            @block.tensor
            def _(pe):
                def fill(job):
                    if index[job]:
                        pe.wait_ge(misc_free, index[job])

                def job_m(job):
                    s = job[1]
                    pe.wait_ge(neg_ready, s + 1)
                    fill(job)
                    for qt in range(TB):
                        ins = pe.transpose(misc[0:MAX_ROWS, qt * P:(qt + 1) * P],
                                           neg_max[:, s % 2, qt].rearrange("p a h -> p (a h)").bitcast(F32), m.ident[:])
                    ins.then_inc(misc_full, 1)

                def job_o(job):
                    pe.wait_ge(out_copied, job[1] + 1)
                    fill(job)
                    for qt in range(TB):
                        ins = pe.transpose(misc[:, qt * P:(qt + 1) * P], out_sb[:, qt * P:(qt + 1) * P], m.ident[:])
                    ins.then_inc(misc_full, 1)

                def job_xt(job):
                    i = job[1]
                    pe.wait_ge(xn_ready, i + 1)
                    fill(job)
                    for c in range(DC):
                        ins = pe.transpose(misc[:, c * P:(c + 1) * P], xn[:, i % 2, c * P:(c + 1) * P], m.ident[:])
                    ins.then_inc(misc_full, 1)

                def job_q1(job):
                    i = job[1]
                    fill(job)
                    for o in range(DC):
                        for c in range(DC):
                            ins = pe.matmul(misc[:, o * P:(o + 1) * P], wq[:, c, o * P:(o + 1) * P], xnt[:, i % 2, c], start=(c == 0), stop=(c == DC - 1))
                    ins.then_inc(misc_full, 1)

                def job_k(job):
                    _, b, o = job
                    pe.wait_ge(ctx_in[b % 2], 16 * n_ctx * (b // 2 + 1))
                    fill(job)
                    for c in range(DC):
                        ins = pe.matmul(misc[:], wk[:, c, o * P:(o + 1) * P], ctx_t[:, b % 2, c], start=(c == 0), stop=(c == DC - 1))
                    ins.then_inc(misc_full, 1)

                def job_v(job):
                    _, b, half = job
                    fill(job)
                    for jj in range(2):
                        j = 2 * half + jj
                        for c in range(DC):
                            ins = pe.matmul(misc[:, jj * D:(jj + 1) * D], ctx_t[:, b % 2, c, j * P:(j + 1) * P], wv[:, c], start=(c == 0), stop=(c == DC - 1))
                    ins.then_inc(misc_full, 1)

                def job_at(job):
                    _, b, c = job
                    fill(job)
                    for qt in range(TB):
                        ins = pe.transpose(misc[:, qt * P:(qt + 1) * P], att[:, b % 2, qt, c * P:(c + 1) * P], m.ident[:])
                    ins.then_inc(misc_full, 1)

                def job_a(job):
                    _, b, half = job
                    fill(job)
                    for jj in range(2):
                        qt = 2 * half + jj
                        for c in range(DC):
                            ins = pe.matmul(misc[:, jj * D:(jj + 1) * D], att_t[:, c, qt * P:(qt + 1) * P], wo[:, c], start=(c == 0), stop=(c == DC - 1))
                    ins.then_inc(misc_full, 1)

                run = {"m": job_m, "o": job_o, "k": job_k, "v": job_v, "at": job_at, "a": job_a,
                       "q": job_xt if layer == 0 else job_q1, "qt": job_xt}

                def maxima_scores(u):
                    s, h = u // HG, u % HG
                    b, g = s // NG, s % NG
                    if h == 0:
                        pe.wait_ge(loaded[g], 96 * (b + 1))
                    for qt in range(TB):
                        n = TB * u + qt
                        if n >= 2:
                            pe.wait_ge(mx_read, n - 1)
                        pe.matmul(m.ps_max[:, n % 2], qa[0:MAX_ROW, g, h, qt * P:(qt + 1) * P], ka[0:MAX_ROW, g, h],
                                  start=True, stop=True).then_inc(mx_full, 1)

                def scores(t):
                    s, kc = t // TB, t % TB
                    b, g = s // NG, s % NG
                    if kc == 0:
                        pe.wait_ge(max_in[g], 16 * (b + 1))
                    for pair in range(2):
                        n = 2 * t + pair
                        if n >= 2:
                            pe.wait_ge(exp_done, n - 1)
                        for hh in range(2):
                            h = 2 * pair + hh
                            ins = pe.matmul(m.ps_st[:, 2 * (n % 2) + hh], ka[0:K_ROWS, g, h, kc * P:(kc + 1) * P], qa[0:K_ROWS, g, h],
                                            start=True, stop=True)
                        ins.then_inc(st_full, 1)

                def weigh(t):
                    s, kc = t // TB, t % TB
                    b, g = s // NG, s % NG
                    pe.wait_ge(exp_done, 2 * t + 2)
                    if kc == 0:
                        pe.wait_ge(v_ready, (b + 1) if layer == 0 else 2 * (b + 1))
                        if s:
                            pe.wait_ge(out_copied, s)
                    for h in range(HG):
                        ins = pe.matmul(m.ps_out[VW * h:VW * (h + 1)], vaug[:, b % 2, kc, HG * g + h], probs[:, t % 3, h],
                                        start=(kc == 0), stop=(kc == TB - 1))
                    ins.then_inc(pv_done, 1)

                pe.wait_ge(m.ident_in, 16)
                if layer == 1:
                    pe.wait_ge(consts_in, 16 * n_const)
                pe.wait_ge(vaug_set, 2)
                for job in jobs[LT[0]]:
                    run[job[0]](job)
                pe.wait_ge(rows_in, 16 * 2 * NG)
                for t in LT[1:]:
                    if 0 <= t < STEPS:
                        scores(t)
                    if 0 <= t + 8 < STEPS:
                        maxima_scores(t + 8)
                    if 0 <= t - 1 < STEPS:
                        weigh(t - 1)
                    for job in jobs[t]:
                        run[job[0]](job)

            @block.scalar
            def _(act):
                def take(job):
                    act.wait_ge(misc_full, index[job] + 1)

                def act_job(job):
                    if job[0] == "m":
                        s = job[1]
                        b, g = s // NG, s % NG
                        if s >= 2:
                            act.wait_ge(max_in[(s - 2) % NG], 16 * ((s - 2) // NG + 1))
                        take(job)
                        nc.scalar.copy(max_t[:, s % 2], misc[0:MAX_ROWS]).then_inc(misc_free, 1)
                        act.wait_ge(misc_free, index[job] + 1)
                        if b >= 1:
                            act.wait_ge(st_full, 8 * (s - NG + 1))
                        act.dma_start(qa[MAX_ROW:K_ROWS, g].bitcast(F32),
                                      max_t[:, s % 2].bitcast(F32).unsqueeze(1).to_broadcast([MAX_ROWS, HG, T])).then_inc(max_in[g], 16)
                    elif job[0] == "qt":
                        take(job)
                        nc.scalar.copy(xnt[:, job[1] % 2], misc[:, 0:D].rearrange("p (c t) -> p c t", c=DC)).then_inc(misc_free, 1)
                    elif job[0] == "k":
                        _, b, o = job
                        if b >= 1:
                            act.wait_ge(k_ready, b)
                        take(job)
                        nc.scalar.activation(kf[:, o], misc[:], ACT.Identity, bias=bqk[:, 1, o:o + 1]).then_inc(misc_free, 1)
                    elif job[0] == "at":
                        _, b, c = job
                        take(job)
                        nc.scalar.copy(att_t[:, c], misc[:]).then_inc(misc_free, 1)

                if layer == 1:
                    act.wait_ge(consts_in, 16 * n_const)
                act.wait_ge(rows_in, 16 * 2 * NG)
                for job in jobs[LT[0]]:
                    act_job(job)
                for t in LT[1:]:
                    if 0 <= t < STEPS:
                        for pair in range(2):
                            n = 2 * t + pair
                            act.wait_ge(st_full, n + 1)
                            if t >= 3:
                                act.wait_ge(pv_done, t - 2)
                            nc.scalar.activation(probs[:, t % 3, 2 * pair:2 * pair + 2], m.ps_st[:, 2 * (n % 2):2 * (n % 2) + 2], ACT.Exp).then_inc(exp_done, 1)
                    if t >= TB and t % TB == 0 and t // TB <= SLOTS:
                        s = t // TB - 1
                        if s:
                            act.wait_ge(misc_full, index["o", s - 1] + 1)
                        act.wait_ge(pv_done, TB * (s + 1))
                        nc.scalar.copy(out_sb[:], m.ps_out[:]).then_inc(out_copied, 1)
                    for job in jobs[t]:
                        act_job(job)

            @block.vector
            def _(dve):
                chain = Counter(dve, dve_chain)

                def take(job):
                    dve.wait_ge(misc_full, index[job] + 1)

                def tile_stats(b):
                    if layer == 0:
                        dve.wait_ge(x_in[b], 16)
                    for j in range(TB):
                        ins = dve.bn_stats(stats[:, j], x[:, TB * b + j])
                    chain.link(ins)
                    for j in range(TB):
                        ins = dve.bn_aggr(mv[:, TB * b + j], stats[:, j])
                    chain.link(ins)
                    rsqrt(dve, chain, rstd[:, TB * b:TB * (b + 1)], mv[:, TB * b:TB * (b + 1), 1],
                          [z[:] for z in tmp], 1.0, LN_EPS)
                    dve.engine_nop().then_inc(stats_done, 1)

                def dve_job(job):
                    if job[0] == "q" and layer == 0:
                        i = job[1]
                        if i >= 2:
                            dve.wait_ge(q_stored[i % 2], 32 * (i // 2))
                        take(job)
                        src = misc[:, 0:D].rearrange("p (c t) -> p c t", c=DC)
                        chain.link(dve.tensor_copy(qst[:, i % 2, 0], src))
                        chain.link(dve.tensor_tensor(qst[:, i % 2, 1], src, qst[:, i % 2, 0].bitcast(F32), ALU.subtract))
                        dve.engine_nop().then_inc(misc_free, 1)
                        dve.engine_nop().then_inc(q_ready, 1)
                    elif job[0] == "q":
                        i = job[1]
                        if i >= 2:
                            dve.wait_ge(q_ready, i - 1)
                        take(job)
                        for o in range(DC):
                            ins = dve.tensor_scalar(qf[:, i % 2, o], misc[:, o * P:(o + 1) * P], bqk[:, 0, o:o + 1], HD ** -0.5, ALU.add, ALU.mult)
                        ins.then_inc(misc_free, 1)
                    elif job[0] == "v":
                        _, b, half = job
                        if b >= 2:
                            dve.wait_ge(pv_done, 16 * (b - 1))
                        take(job)
                        chain.link(dve.tensor_tensor(
                            vaug[:, b % 2, 2 * half:2 * half + 2, :, 0:HD],
                            misc[:].rearrange("p (j h d) -> p j h d", j=2, d=HD),
                            bv[:].rearrange("p (h d) -> p h d", d=HD).unsqueeze(1).to_broadcast([P, 2, H, HD]), ALU.add))
                        dve.engine_nop().then_inc(misc_free, 1)
                        dve.engine_nop().then_inc(v_ready, 1)
                        if half == 1:
                            dve.engine_nop().then_inc(ctx_used, 1)
                    elif job[0] == "o":
                        s = job[1]
                        b, g = s // NG, s % NG
                        take(job)
                        o = misc[:].rearrange("p (j h w) -> p j h w", j=TB, w=VW)
                        chain.link(dve.reciprocal(rden[:], o[:, :, :, HD]))
                        if layer == 0:
                            dst = att[:, s % 2].rearrange("p j (h d) -> p j h d", d=HD)
                            if s >= 2:
                                dve.wait_ge(att_added, s - 1)
                        else:
                            dst = att[:, b % 2, :, g * HG * HD:(g + 1) * HG * HD].rearrange("p j (h d) -> p j h d", d=HD)
                        dve.tensor_tensor(dst, o[:, :, :, 0:HD], rden[:].unsqueeze(3).to_broadcast([P, TB, HG, HD]), ALU.mult).then_inc(misc_free, 1)
                    elif job[0] == "a":
                        _, b, half = job
                        take(job)
                        xs = x[:, TB * b + 2 * half:TB * b + 2 * half + 2]
                        dve.tensor_tensor(xs, misc[:].rearrange("p (j d) -> p j d", j=2), xs, ALU.add).then_inc(misc_free, 1)

                def maxima(u):
                    s, h = u // HG, u % HG
                    for qt in range(TB):
                        n = TB * u + qt
                        dve.wait_ge(mx_full, n + 1)
                        dve.tensor_reduce(row_max[:, s % 3, h, qt:qt + 1], m.ps_max[:, n % 2], AX.X, ALU.max).then_inc(mx_read, 1)
                    if h == HG - 1:
                        dve.wait_ge(mx_read, TB * (u + 1))
                        if s >= 2:
                            dve.wait_ge(misc_full, index["m", s - 2] + 1)
                        src = row_max[:, s % 3].rearrange("p h j -> p j h")
                        chain.link(dve.tensor_scalar(neg_max[:, s % 2, :, 0], src, -1.0, None, ALU.mult))
                        dve.scalar_tensor_tensor(neg_max[:, s % 2, :, 1], src, -1.0, neg_max[:, s % 2, :, 0].bitcast(F32),
                                                 ALU.mult, ALU.subtract).then_inc(neg_ready, 1)

                tile_stats(0)
                dve.memset(vaug[:, :, :, :, HD:HD + 1], 1.0).then_inc(vaug_set, 1)
                dve.memset(vaug[:, :, :, :, HD + 1:VW], 0.0).then_inc(vaug_set, 1)
                if layer == 1:
                    dve.wait_ge(consts_in, 16 * n_const)
                for job in jobs[LT[0]]:
                    dve_job(job)
                for b in range(1, B):
                    tile_stats(b)
                for t in LT[1:]:
                    if 0 <= t + 8 < STEPS:
                        maxima(t + 8)
                    for job in jobs[t]:
                        dve_job(job)


def moe_top1(nc, m, dram):
    with ExitStack() as ctx:
        def sb(name, shape, dt):
            return ctx.enter_context(nc.sbuf_tensor(f"e0_{name}", shape, dt))

        def sem(name):
            return m.ctx.enter_context(nc.semaphore(f"e0_{name}"))

        x = m.x
        xn = sb("xn", [P, NT, D], F32)
        sq = sb("sq", [P, D], F32)
        xnt = sb("xnt", [P, 2, DC, P], F32)
        rms_w = sb("rms_w", [P, D], F32)
        gate = sb("gate", [P, DC, E], F32)
        upper = sb("upper", [P, P], F32)
        tie = sb("tie", [P, E], F32)
        steps = sb("steps", [P, NT], F32)
        before = sb("before", [P, E, E], F32)
        tile_no = sb("tile_no", [P, SEL_TILES], F32)
        upper_b = sb("upper_b", [P, P], BF16)
        ones_b = sb("ones_b", [P, P], BF16)
        zero = sb("zero", [P, D], F32)
        stats = sb("stats", [P, NT, 6], F32)
        mv = sb("mv", [P, NT, 2], F32)
        rstd = sb("rstd", [P, NT], F32)
        ms = sb("ms", [P, NT], F32)
        rrms = sb("rrms", [P, NT], F32)
        tmp = [sb(f"tmp{i}", [P, NT], F32) for i in range(2)]
        logits = sb("logits", [P, NT, E], F32)
        prob = sb("prob", [P, NT, E], F32)
        work = sb("work", [P, NT, E], F32)
        top = sb("top", [P, NT], F32)
        score = sb("score", [P, NT], F32)
        onehot = sb("onehot", [P, NT, E], F32)
        onehot_b = sb("onehot_b", [P, NT, E], BF16)
        count = sb("count", [P, E], F32)
        tiles_e = sb("tiles_e", [P, E], F32)
        base = sb("base", [P, E], F32)
        last = sb("last", [P, E], F32)
        cmp = sb("cmp", [P, E, NT], F32)
        pre = sb("pre", [P, E, E], F32)
        which = sb("which", [P, SEL_TILES, E], F32)
        expert_f = sb("expert_f", [P, SEL_TILES], F32)
        expert = sb("expert", [P, SEL_TILES], I32)
        slot_f = sb("slot_f", [P, NT], F32)
        slot = sb("slot", [P, NT], U32)
        wts = sb("wts", [P, 2, W0_COLS], F32)
        xs = sb("xs", [P, 2, D], F32)
        xst = sb("xst", [P, 2, DC, P], F32)
        hid = sb("hid", [P, 2, FC, P], F32)
        ys = sb("ys", [P, 2, D], F32)
        yg = sb("yg", [P, 2, D], F32)

        consts_in = sem("consts_in")
        zero_set = sem("zero_set")
        zeroed = sem("zeroed")
        ln_done = sem("ln_done")
        xl_ready = sem("xl_ready")
        sq_done = sem("sq_done")
        xn_ready = sem("xn_ready")
        xt_full = sem("xt_full")
        xt_copied = sem("xt_copied")
        logits_full = sem("logits_full")
        max_off = sem("max_off")
        exp_done = sem("exp_done")
        onehot_ready = sem("onehot_ready")
        ranks_full = sem("ranks_full")
        routed = sem("routed")
        scattered = sem("scattered")
        xs_in = [sem(f"xs_in{i}") for i in range(2)]
        w1_in = [sem(f"w1_in{i}") for i in range(2)]
        w2_in = [sem(f"w2_in{i}") for i in range(2)]
        h_full = sem("h_full")
        xst_full = sem("xst_full")
        xst_ready = sem("xst_ready")
        hid_ready = sem("hid_ready")
        y_full = sem("y_full")
        y_copied = sem("y_copied")
        y_stored = [sem(f"y_stored{i}") for i in range(2)]
        gathered = [sem(f"gathered{i}") for i in range(2)]
        added = sem("added")
        dve_chain = sem("dve_chain")

        consts = ((rms_w, "rms_w"), (gate, "gate0"), (upper, "upper"), (tie, "tie"), (steps, "steps"), (before, "before"), (tile_no, "tile_no"))
        w1_cols = DC * F
        n_tiles = SEL_TILES

        with nc.Block() as block:

            @block.sync
            def _(sp):
                for dst, src in consts:
                    sp.dma_start(dst[:], dram[src]).then_inc(consts_in, 16)
                sp.wait_ge(zero_set, 1)
                sp.dma_start(dram["xs"].rearrange("(n p) d -> p n d", p=P), zero[:].unsqueeze(1).to_broadcast([P, n_tiles + 1, D])).then_inc(zeroed, 16)
                sp.wait_ge(routed, 1)
                sp.wait_ge(scattered, 16 * NT)
                xs_dram = dram["xs"].rearrange("(n p) d -> n p d", p=P)
                sp.dma_start(xs[:, 0], xs_dram[0]).then_inc(xs_in[0], 16)
                def turn_of_loop(i):
                    for k in range(2):
                        n = i * 2 + k
                        e = sp.value_load(expert[0:1, bass.ds(n, 1)], min_val=0, max_val=E - 1)
                        wait_from(sp, h_full, 2 * n - 2)
                        sp.dma_start(wts[:, k, 0:w1_cols], dram["w0"][bass.ds(e, 1), :, 0:w1_cols].rearrange("a p f -> (a p) f")).then_inc(w1_in[k], 16)
                        wait_from(sp, y_copied, n - 1)
                        sp.dma_start(wts[:, k, w1_cols:], dram["w0"][bass.ds(e, 1), :, w1_cols:].rearrange("a p f -> (a p) f")).then_inc(w2_in[k], 16)
                        wait_from(sp, xst_full, n)
                        sp.dma_start(xs[:, 1 - k], xs_dram[bass.ds(n + 1, 1)].rearrange("a p d -> (a p) d")).then_inc(xs_in[1 - k], 16)

                turns(sp, n_tiles // 2, turn_of_loop)
                for k in range(2):
                    sp.wait_ge(y_stored[k], 16 * (n_tiles // 2))

            @block.gpsimd
            def _(pool):
                pool.memset(zero[:], 0.0).then_inc(zero_set, 1)
                for i in range(NT):
                    pool.wait_ge(ln_done, 1)
                    pool.tensor_scalar(xn[:, i], x[:, i], mv[:, i, 0:1], rstd[:, i:i + 1], ALU.subtract, ALU.mult).then_inc(xl_ready, 1)
                pool.wait_ge(zeroed, 16)
                pool.wait_ge(routed, 1)
                for i in range(NT):
                    pool.indirect_dma_start(dram["xs"], bass.IndirectOffsetOnAxis(slot[:, i:i + 1], 0), xn[:, i], None).then_inc(scattered, 16)
                def turn_of_loop(it):
                    for k in range(2):
                        n = it * 2 + k
                        pool.wait_ge(y_copied, n + 1)
                        pool.dma_start(dram["ys"].rearrange("(n p) d -> n p d", p=P)[bass.ds(n, 1)].rearrange("a p d -> (a p) d"), ys[:, k]).then_inc(y_stored[k], 16)

                turns(pool, n_tiles // 2, turn_of_loop)
                for k in range(2):
                    pool.wait_ge(y_stored[k], 16 * (n_tiles // 2))
                for i in range(NT):
                    if i >= 2:
                        pool.wait_ge(added, i - 1)
                    pool.indirect_dma_start(yg[:, i % 2], None, dram["ys"], bass.IndirectOffsetOnAxis(slot[:, i:i + 1], 0)).then_inc(gathered[i % 2], 16)

            @block.scalar
            def _(act):
                for i in range(NT):
                    act.wait_ge(xl_ready, i + 1)
                    if i:
                        act.wait_ge(sq_done, i)
                    nc.scalar.activation(sq[:], xn[:, i], ACT.Square, accum_out=ms[:, i:i + 1]).then_inc(sq_done, 1)
                for i in range(NT):
                    act.wait_ge(xt_full, i + 1)
                    if i >= 2:
                        act.wait_ge(logits_full, i - 1)
                    nc.scalar.copy(xnt[:, i % 2], m.ps_max[:, i % 2, 0:D].rearrange("p (c t) -> p c t", c=DC)).then_inc(xt_copied, 1)
                act.wait_ge(max_off, 1)
                nc.scalar.activation(prob[:], work[:], ACT.Exp).then_inc(exp_done, 1)
                def turn_of_loop(it):
                    for k in range(2):
                        n = it * 2 + k
                        act.wait_ge(w2_in[k], 16 * it + 16)
                        wait_from(act, y_full, n - 1)
                        for half in range(2):
                            act.wait_ge(h_full, 2 * n + half + 1)
                            for q in range(4):
                                fc = 4 * half + q
                                nc.scalar.activation(hid[:, k, fc], m.ps_st[:, 2 * k + half, q * P:(q + 1) * P], ACT.Silu,
                                                     bias=wts[:, k, w1_cols + FC * D + fc:w1_cols + FC * D + fc + 1]).then_inc(hid_ready, 1)

                turns(act, n_tiles // 2, turn_of_loop)
            @block.tensor
            def _(pe):
                for i in range(NT + 1):
                    if i < NT:
                        pe.wait_ge(xn_ready, i + 1)
                        if i >= 2:
                            pe.wait_ge(xt_copied, i - 1)
                        for c in range(DC):
                            ins = pe.transpose(m.ps_max[:, i % 2, c * P:(c + 1) * P], xn[:, i, c * P:(c + 1) * P], m.ident[:])
                        ins.then_inc(xt_full, 1)
                    if i == 0:
                        pe.wait_ge(consts_in, 16 * len(consts))
                        continue
                    pe.wait_ge(xt_copied, i)
                    for c in range(DC):
                        ins = pe.matmul(m.ps_out[:, (i - 1) * E:i * E], xnt[:, (i - 1) % 2, c], gate[:, c], start=(c == 0), stop=(c == DC - 1))
                    ins.then_inc(logits_full, 1)
                pe.wait_ge(onehot_ready, 1)
                flat = onehot_b[:].rearrange("p n e -> p (n e)")
                for i in range(NT - 1):
                    pe.matmul(m.ps_misc[:, (i + 1) * E:NT * E].rearrange("p (n e) -> p n e", e=E), ones_b[:],
                              onehot_b[:, i:i + 1].to_broadcast([P, NT - 1 - i, E]), start=(i == 0), stop=False, skip_group_check=True)
                pe.matmul(m.ps_misc[:, 0:NT * E], upper_b[:], flat, start=False, stop=True, skip_group_check=True)
                for i in range(NT):
                    ins = pe.matmul(m.ps_max[:, 0, 0:E], ones_b[:], onehot_b[:, i], start=(i == 0), stop=(i == NT - 1))
                ins.then_inc(ranks_full, 1)

                def turn(k):
                    for c in range(DC):
                        ins = pe.transpose(m.ps_misc[:, c * P:(c + 1) * P], xs[:, k, c * P:(c + 1) * P], m.ident[:])
                    return ins

                pe.wait_ge(xs_in[0], 16)
                ins = turn(0)
                ins.then_inc(xst_full, 1)
                def turn_of_loop(it):
                    for k in range(2):
                        n = it * 2 + k
                        pe.wait_ge(w1_in[k], 16 * it + 16)
                        pe.wait_ge(xst_ready, n + 1)
                        for half in range(2):
                            wait_from(pe, hid_ready, 8 * n - 12 + 4 * half)
                            for q in range(4):
                                fc = 4 * half + q
                                for c in range(DC):
                                    ins = pe.matmul(m.ps_st[:, 2 * k + half, q * P:(q + 1) * P], wts[:, k, c * F + fc * P:c * F + (fc + 1) * P], xst[:, k, c],
                                                    start=(c == 0), stop=(c == DC - 1))
                            ins.then_inc(h_full, 1)
                        pe.wait_ge(xs_in[1 - k], (16 * it + 16) if k == 0 else (16 * it + 32))
                        turn(1 - k).then_inc(xst_full, 1)
                        pe.wait_ge(w2_in[k], 16 * it + 16)
                        wait_from(pe, y_copied, n - 1)
                        for fc in range(FC):
                            if fc % 4 == 0:
                                pe.wait_ge(hid_ready, 8 * n + 4 + fc)
                            ins = pe.matmul(m.ps_max[:, k, 0:D], hid[:, k, fc], wts[:, k, w1_cols + fc * D:w1_cols + (fc + 1) * D], start=(fc == 0), stop=(fc == FC - 1))
                        ins.then_inc(y_full, 1)

                turns(pe, n_tiles // 2, turn_of_loop)
            @block.vector
            def _(dve):
                chain = Counter(dve, dve_chain)
                dve.memset(ones_b[:], 1.0)
                for i in range(NT):
                    ins = dve.bn_stats(stats[:, i], x[:, i])
                chain.link(ins)
                for i in range(NT):
                    ins = dve.bn_aggr(mv[:, i], stats[:, i])
                chain.link(ins)
                rsqrt(dve, chain, rstd[:], mv[:, :, 1], [z[:] for z in tmp], 1.0, LN_EPS)
                dve.engine_nop().then_inc(ln_done, 1)
                dve.wait_ge(consts_in, 16 * len(consts))
                dve.tensor_copy(upper_b[:], upper[:])
                dve.wait_ge(sq_done, NT)
                rsqrt(dve, chain, rrms[:], ms[:], [z[:] for z in tmp], 1.0 / D, RMS_EPS)
                for i in range(NT):
                    dve.wait_ge(xl_ready, i + 1)
                    dve.scalar_tensor_tensor(xn[:, i], xn[:, i], rrms[:, i:i + 1], rms_w[:], ALU.mult, ALU.mult).then_inc(xn_ready, 1)
                dve.wait_ge(logits_full, NT)
                lg = m.ps_out[:, 0:NT * E].rearrange("p (n e) -> p n e", e=E)
                chain.link(dve.tensor_copy(logits[:], lg))
                chain.link(dve.tensor_reduce(top[:], logits[:], AX.X, ALU.max))
                dve.tensor_tensor(work[:], logits[:], top[:].unsqueeze(2).to_broadcast([P, NT, E]), ALU.subtract).then_inc(max_off, 1)
                dve.wait_ge(exp_done, 1)
                chain.link(dve.tensor_reduce(score[:], prob[:], AX.X, ALU.add))
                chain.link(dve.reciprocal(score[:], score[:]))
                chain.link(dve.tensor_tensor(prob[:], prob[:], score[:].unsqueeze(2).to_broadcast([P, NT, E]), ALU.mult))
                chain.link(dve.tensor_reduce(score[:], prob[:], AX.X, ALU.max))
                chain.link(dve.tensor_tensor(work[:], prob[:], score[:].unsqueeze(2).to_broadcast([P, NT, E]), ALU.is_ge))
                chain.link(dve.tensor_tensor(work[:], work[:], tie[:].unsqueeze(1).to_broadcast([P, NT, E]), ALU.mult))
                chain.link(dve.tensor_reduce(top[:], work[:], AX.X, ALU.max))
                chain.link(dve.tensor_tensor(onehot[:], work[:], top[:].unsqueeze(2).to_broadcast([P, NT, E]), ALU.is_equal))
                dve.tensor_copy(onehot_b[:], onehot[:]).then_inc(onehot_ready, 1)
                dve.wait_ge(ranks_full, 1)
                chain.link(dve.tensor_copy(count[:], m.ps_max[:, 0, 0:E]))
                chain.link(dve.tensor_tensor(cmp[:], count[:].unsqueeze(2).to_broadcast([P, E, NT]), steps[:].unsqueeze(1).to_broadcast([P, E, NT]), ALU.is_gt))
                chain.link(dve.tensor_reduce(tiles_e[:], cmp[:], AX.X, ALU.add))
                chain.link(dve.tensor_tensor(pre[:], before[:], tiles_e[:].unsqueeze(1).to_broadcast([P, E, E]), ALU.mult))
                chain.link(dve.tensor_reduce(base[:], pre[:], AX.X, ALU.add))
                chain.link(dve.tensor_tensor(last[:], base[:], tiles_e[:], ALU.add))
                chain.link(dve.tensor_scalar(base[:], base[:], float(P), None, ALU.mult))
                rank = m.ps_misc[:, 0:NT * E].rearrange("p (n e) -> p n e", e=E)
                chain.link(dve.tensor_tensor(work[:], rank, base[:].unsqueeze(1).to_broadcast([P, NT, E]), ALU.add))
                chain.link(dve.tensor_tensor(work[:], work[:], onehot[:], ALU.mult))
                chain.link(dve.tensor_reduce(slot_f[:], work[:], AX.X, ALU.add))
                chain.link(dve.tensor_copy(slot[:], slot_f[:]))
                chain.link(dve.tensor_tensor(which[:], last[:].unsqueeze(1).to_broadcast([P, SEL_TILES, E]), tile_no[:].unsqueeze(2).to_broadcast([P, SEL_TILES, E]), ALU.is_le))
                chain.link(dve.tensor_reduce(expert_f[:], which[:], AX.X, ALU.add))
                chain.link(dve.tensor_scalar(expert[:], expert_f[:], float(E - 1), None, ALU.min))
                dve.engine_nop().then_inc(routed, 1)
                dve.wait_ge(xst_full, 1)
                dve.tensor_copy(xst[:, 0], m.ps_misc[:, 0:D].rearrange("p (c t) -> p c t", c=DC)).then_inc(xst_ready, 1)
                def turn_of_loop(it):
                    for k in range(2):
                        n = it * 2 + k
                        dve.wait_ge(xst_full, n + 2)
                        dve.tensor_copy(xst[:, 1 - k], m.ps_misc[:, 0:D].rearrange("p (c t) -> p c t", c=DC)).then_inc(xst_ready, 1)
                        dve.wait_ge(y_full, n + 1)
                        wait_from(dve, y_stored[k], 16 * it)
                        dve.tensor_tensor(ys[:, k], m.ps_max[:, k, 0:D], wts[:, k, W0_COLS - D:W0_COLS], ALU.add).then_inc(y_copied, 1)

                turns(dve, n_tiles // 2, turn_of_loop)
                for i in range(NT):
                    dve.wait_ge(gathered[i % 2], 16 * (i // 2 + 1))
                    dve.scalar_tensor_tensor(x[:, i], yg[:, i % 2], score[:, i:i + 1], x[:, i], ALU.mult, ALU.add).then_inc(added, 1)


def moe_top_k(nc, m, dram):
    with ExitStack() as ctx:
        def sb(name, shape, dt):
            return ctx.enter_context(nc.sbuf_tensor(f"e1_{name}", shape, dt))

        def sem(name):
            return m.ctx.enter_context(nc.semaphore(f"e1_{name}"))

        x = m.x
        NE = B * E
        xn = sb("xn", [P, NT, D], F32)
        xnt = sb("xnt", [P, 2, DC, P], F32)
        gate = sb("gate", [P, DC, E], F32)
        row_base = sb("row_base", [NE, 1], F32)
        zero = sb("zero", [P, D], F32)
        stats = sb("stats", [P, NT, 6], F32)
        mv = sb("mv", [P, NT, 2], F32)
        rstd = sb("rstd", [P, NT], F32)
        tmp = [sb(f"tmp{i}", [P, NT], F32) for i in range(2)]
        work = sb("work", [P, NT, E], F32)
        prob = sb("prob", [P, NT, E], F32)
        top = sb("top", [P, NT], F32)
        prob_j = sb("prob_j", [P, TB, B, E], F32)
        rows = sb("rows", [NE, 2, T], F32)
        best = sb("best", [NE, CAP], F32)
        best_at = sb("best_at", [NE, CAP], U32)
        best_tok = sb("best_tok", [NE, CAP], F32)
        gate_w = sb("gate_w", [P, B, E], F32)
        token = sb("token", [P, E + 1, B], U32)
        token_e = sb("token_e", [P, 2, B], U32)
        token_s = sb("token_s", [P, 2, B], U32)
        xg = sb("xg", [P, 2, B, D], F32)
        xt = sb("xt", [P, 2, DC, B * CAP], F32R)
        wf = sb("wf", [P, 2 * DC * F], F32)
        wr = sb("wr", [P, 2, 2 * DC * F], F32R)
        hf = sb("hf", [P, 2, B * CAP], F32)
        hr = sb("hr", [P, 2, FC, B * CAP], F32R)
        ys = sb("ys", [P, 2, B, D], F32)
        half_b = sb("half_b", [P, 2, TB, D], BF16)

        consts_in = sem("consts_in")
        zero_set = sem("zero_set")
        zeroed = sem("zeroed")
        xn_ready = sem("xn_ready")
        xn_stored = sem("xn_stored")
        xt_full = sem("xt_full")
        xt_copied = sem("xt_copied")
        logits_full = sem("logits_full")
        max_off = sem("max_off")
        exp_done = sem("exp_done")
        prob_ready = sem("prob_ready")
        rows_full = sem("rows_full")
        picked = sem("picked")
        picks_full = sem("picks_full")
        routed = sem("routed")
        token_ready = sem("token_ready")
        gathered = [sem(f"gathered{i}") for i in range(2)]
        w_in = [sem(f"w_in{i}") for i in range(2)]
        w_hi = [sem(f"w_hi{i}") for i in range(2)]
        w_lo = [sem(f"w_lo{i}") for i in range(2)]
        x_hi = sem("x_hi")
        h_hi = sem("h_hi")
        scatter_ready = sem("scatter_ready")
        waited = sem("waited")
        x_full = sem("x_full")
        x_split = sem("x_split")
        h_full = sem("h_full")
        h_copied = sem("h_copied")
        h_split = sem("h_split")
        y_full = sem("y_full")
        y_copied = sem("y_copied")
        y_added = [sem(f"y_added{i}") for i in range(2)]
        sum_in = sem("sum_in")
        out_ready = sem("out_ready")
        out_stored = sem("out_stored")
        dve_chain = sem("dve_chain")
        HALF = DC * F
        y_bank = (m.ps_out, m.ps_misc)

        with nc.Block() as block:

            @block.sync
            def _(sp):
                sp.dma_start(gate[:], dram["gate1"]).then_inc(consts_in, 16)
                sp.dma_start(row_base[:], dram["row_base"]).then_inc(consts_in, 16)
                sp.wait_ge(zero_set, 1)
                sp.dma_start(dram["acc"].rearrange("(n p) d -> p n d", p=P), zero[:].unsqueeze(1).to_broadcast([P, NT, D])).then_inc(zeroed, 16)
                for b in range(B):
                    sp.wait_ge(xn_ready, TB * (b + 1))
                    sp.dma_start(dram["xl"][b * T:(b + 1) * T].rearrange("(n p) d -> p n d", p=P), xn[:, TB * b:TB * (b + 1)]).then_inc(xn_stored, 16)
                def turn_of_loop(e):
                    for part in range(2):
                        wait_from(sp, w_lo[part], e)
                        sp.dma_start(wf[:, part * HALF:(part + 1) * HALF], dram["w1"][bass.ds(e, 1), :, part * HALF:(part + 1) * HALF].rearrange("a p f -> (a p) f")).then_inc(w_in[part], 16)

                turns(sp, E, turn_of_loop)
                for k in range(2):
                    sp.wait_ge(y_added[k], 16 * B * (E // 2))
                sp.dma_start(xn[:], dram["acc"].rearrange("(n p) d -> p n d", p=P)).then_inc(sum_in, 16)
                for b in range(B):
                    sp.wait_ge(out_ready, b + 1)
                    sp.dma_start(dram["out"][b].rearrange("(j p) d -> p j d", p=P), x[:, TB * b:TB * (b + 1)]).then_inc(out_stored, 16)
                sp.wait_ge(out_stored, 16 * B)

            @block.gpsimd
            def _(pool):
                pool.memset(zero[:], 0.0).then_inc(zero_set, 1)
                pool.wait_ge(routed, 1)
                pool.wait_ge(xn_stored, 16 * B)
                pool.wait_ge(zeroed, 16)

                def gather(e, k):
                    pool.tensor_copy(token_e[:, k].unsqueeze(1), token[:, bass.ds(e, 1)]).then_inc(token_ready, 1)
                    pool.wait_ge(token_ready, e + 1)
                    pool.sem_inc(waited, 1)
                    for b in range(B):
                        pool.indirect_dma_start(xg[:, k, b], None, dram["xl"], bass.IndirectOffsetOnAxis(token_e[:, k, b:b + 1], 0)).then_inc(gathered[k], 16)

                def scatter(e, it, k):
                    pool.wait_ge(y_copied, B * e + B)
                    wait_from(pool, y_added[1 - k], 16 * B * (it + k))
                    pool.sem_inc(waited, 1)
                    for b in range(B):
                        pool.indirect_dma_start(dram["acc"], bass.IndirectOffsetOnAxis(token_s[:, k, b:b + 1], 0), ys[:, k, b], None,
                                                compute_op=ALU.add).then_inc(y_added[k], 16)

                def low_part(part, e):
                    pool.wait_ge(w_hi[part], e + 1)
                    cols = slice(part * HALF, (part + 1) * HALF)
                    pool.tensor_tensor(wr[:, 1, cols], wf[:, cols], wr[:, 0, cols].bitcast(F32), ALU.subtract).then_inc(w_lo[part], 1)

                def turn_of_loop(it):
                    for k in range(2):
                        e = it * 2 + k
                        low_part(0, e)
                        wait_from(pool, x_full, e)
                        gather(e + 1, 1 - k)
                        low_part(1, e)
                        if not isinstance(e, int) or e > 0:
                            pool.tensor_copy(token_s[:, 1 - k].unsqueeze(1), token[:, bass.ds(e - 1, 1)]).then_inc(scatter_ready, 1)
                            pool.wait_ge(scatter_ready, e)
                            scatter(e - 1, it + k - 1, 1 - k)

                gather(0, 0)
                turns(pool, E // 2, turn_of_loop)
                pool.tensor_copy(token_s[:, 1].unsqueeze(1), token[:, E - 1:E]).then_inc(scatter_ready, 1)
                pool.wait_ge(scatter_ready, E)
                scatter(E - 1, E // 2 - 1, 1)

            @block.scalar
            def _(act):
                for i in range(NT):
                    act.wait_ge(xt_full, i + 1)
                    if i >= 2:
                        act.wait_ge(logits_full, i - 1)
                    nc.scalar.copy(xnt[:, i % 2], m.ps_max[:, i % 2, 0:D].rearrange("p (c t) -> p c t", c=DC)).then_inc(xt_copied, 1)
                act.wait_ge(max_off, 1)
                nc.scalar.activation(prob[:], work[:], ACT.Exp).then_inc(exp_done, 1)
                def turn_of_loop(e):
                    for part, (used, n) in enumerate(((h_full, FC), (y_full, B))):
                        act.wait_ge(w_in[part], 16 * e + 16)
                        wait_from(act, used, n * e)
                        cols = slice(part * HALF, (part + 1) * HALF)
                        nc.scalar.copy(wr[:, 0, cols], wf[:, cols]).then_inc(w_hi[part], 1)
                    for fc in range(FC):
                        act.wait_ge(h_full, FC * e + fc + 1)
                        wait_from(act, h_split, FC * e + fc - 1)
                        nc.scalar.activation(hf[:, fc % 2], m.ps_st[:, fc % 4], ACT.Gelu_apprx_tanh).then_inc(h_copied, 1)

                turns(act, E, turn_of_loop)
            @block.tensor
            def _(pe):
                for i in range(NT + 1):
                    if i < NT:
                        pe.wait_ge(xn_ready, i + 1)
                        if i >= 2:
                            pe.wait_ge(xt_copied, i - 1)
                        for c in range(DC):
                            ins = pe.transpose(m.ps_max[:, i % 2, c * P:(c + 1) * P], xn[:, i, c * P:(c + 1) * P], m.ident[:])
                        ins.then_inc(xt_full, 1)
                    if i == 0:
                        pe.wait_ge(consts_in, 32)
                        continue
                    pe.wait_ge(xt_copied, i)
                    for c in range(DC):
                        ins = pe.matmul(m.ps_out[:, (i - 1) * E:i * E], xnt[:, (i - 1) % 2, c], gate[:, c], start=(c == 0), stop=(c == DC - 1))
                    ins.then_inc(logits_full, 1)
                pe.wait_ge(prob_ready, 1)
                for j in range(TB):
                    ins = pe.transpose(m.ps_misc[0:NE, j * P:(j + 1) * P], prob_j[:, j].rearrange("p b e -> p (b e)"), m.ident[:])
                ins.then_inc(rows_full, 1)
                pe.wait_ge(picked, 1)
                pe.transpose(m.ps_misc[:, 0:NE], best_tok[:], m.ident[0:NE, 0:NE])
                pe.transpose(m.ps_misc[:, NE:2 * NE], best[:], m.ident[0:NE, 0:NE]).then_inc(picks_full, 1)

                def turn(k):
                    for c in range(DC):
                        for b in range(B):
                            ins = pe.transpose(m.ps_max[:, c, b * P:(b + 1) * P], xg[:, k, b, c * P:(c + 1) * P], m.ident[:])
                    ins.then_inc(x_full, 1)

                pe.wait_ge(gathered[0], 16 * B)
                turn(0)
                terms = ((0, 0), (1, 0), (0, 1))
                def turn_of_loop(it):
                    for k in range(2):
                        e = it * 2 + k
                        pe.wait_ge(w_lo[0], e + 1)
                        pe.wait_ge(x_split, e + 1)
                        for fc in range(FC):
                            wait_from(pe, h_copied, FC * e + fc - 3)
                            for c in range(DC):
                                for wp, xp in terms:
                                    ins = pe.matmul(m.ps_st[:, fc % 4], wr[:, wp, c * F + fc * P:c * F + (fc + 1) * P], xt[:, xp, c],
                                                    start=(c == 0 and (wp, xp) == (0, 0)), stop=(c == DC - 1 and (wp, xp) == (0, 1)))
                            ins.then_inc(h_full, 1)
                        pe.wait_ge(gathered[1 - k], (16 * B * it + 16 * B) if k == 0 else (16 * B * it + 32 * B))
                        turn(1 - k)
                        pe.wait_ge(w_lo[1], e + 1)
                        for b in range(B):
                            wait_from(pe, y_copied, B * e + b - 1)
                            for fc in range(FC):
                                if b == 0:
                                    pe.wait_ge(h_split, FC * e + fc + 1)
                                for hp, wp in terms:
                                    ins = pe.matmul(y_bank[b % 2][:, 0:D], hr[:, hp, fc, b * P:(b + 1) * P], wr[:, wp, HALF + fc * D:HALF + (fc + 1) * D],
                                                    start=(fc == 0 and (hp, wp) == (0, 0)), stop=(fc == FC - 1 and (hp, wp) == (0, 1)))
                            ins.then_inc(y_full, 1)

                turns(pe, E // 2, turn_of_loop)
            @block.vector
            def _(dve):
                chain = Counter(dve, dve_chain)
                for i in range(NT):
                    ins = dve.bn_stats(stats[:, i], x[:, i])
                chain.link(ins)
                for i in range(NT):
                    ins = dve.bn_aggr(mv[:, i], stats[:, i])
                chain.link(ins)
                rsqrt(dve, chain, rstd[:], mv[:, :, 1], [z[:] for z in tmp], 1.0, LN_EPS)
                for i in range(NT):
                    dve.tensor_scalar(xn[:, i], x[:, i], mv[:, i, 0:1], rstd[:, i:i + 1], ALU.subtract, ALU.mult).then_inc(xn_ready, 1)
                dve.wait_ge(logits_full, NT)
                lg = m.ps_out[:, 0:NT * E].rearrange("p (n e) -> p n e", e=E)
                chain.link(dve.tensor_reduce(top[:], lg, AX.X, ALU.max))
                dve.tensor_tensor(work[:], lg, top[:].unsqueeze(2).to_broadcast([P, NT, E]), ALU.subtract).then_inc(max_off, 1)
                dve.wait_ge(exp_done, 1)
                chain.link(dve.tensor_reduce(top[:], prob[:], AX.X, ALU.add))
                chain.link(dve.reciprocal(top[:], top[:]))
                dve.tensor_tensor(prob_j[:].rearrange("p j b e -> p b j e"), prob[:].rearrange("p (b j) e -> p b j e", b=B),
                                  top[:].rearrange("p (b j) -> p b j", b=B).unsqueeze(3).to_broadcast([P, B, TB, E]), ALU.mult).then_inc(prob_ready, 1)
                dve.wait_ge(rows_full, 1)
                chain.link(dve.tensor_copy(rows[:, 0], m.ps_misc[0:NE]))
                for r in range(CAP // 8):
                    cols = slice(8 * r, 8 * r + 8)
                    chain.link(dve.max(best[:, cols], rows[:, r % 2]))
                    chain.link(dve.max_index(best_at[:, cols], best[:, cols], rows[:, r % 2]))
                    if r < CAP // 8 - 1:
                        chain.link(dve.match_replace(rows[:, (r + 1) % 2], best[:, cols], rows[:, r % 2], -1.0))
                dve.wait_ge(consts_in, 32)
                dve.tensor_scalar(best_tok[:], best_at[:], row_base[:], None, ALU.add).then_inc(picked, 1)
                dve.wait_ge(picks_full, 1)
                chain.link(dve.tensor_copy(token[:, 0:E].rearrange("p e b -> p b e"), m.ps_misc[:, 0:NE].rearrange("p (b e) -> p b e", e=E)))
                dve.tensor_copy(token[:, E], token[:, 0])
                chain.link(dve.tensor_copy(gate_w[:], m.ps_misc[:, NE:2 * NE].rearrange("p (b e) -> p b e", e=E)))
                dve.engine_nop().then_inc(routed, 1)

                def split_x(e):
                    dve.wait_ge(x_full, e + 1)
                    dve.tensor_copy(xt[:, 0], m.ps_max[:]).then_inc(x_hi, 1)
                    dve.wait_ge(x_hi, e + 1)
                    dve.tensor_tensor(xt[:, 1], m.ps_max[:], xt[:, 0].bitcast(F32), ALU.subtract).then_inc(x_split, 1)

                split_x(0)
                def turn_of_loop(it):
                    for k in range(2):
                        e = it * 2 + k
                        for fc in range(FC):
                            dve.wait_ge(h_copied, FC * e + fc + 1)
                            dve.tensor_copy(hr[:, 0, fc], hf[:, fc % 2]).then_inc(h_hi, 1)
                            dve.wait_ge(h_hi, FC * e + fc + 1)
                            dve.tensor_tensor(hr[:, 1, fc], hf[:, fc % 2], hr[:, 0, fc].bitcast(F32), ALU.subtract).then_inc(h_split, 1)
                        split_x(e + 1)
                        wait_from(dve, y_added[k], 16 * B * it)
                        for b in range(B):
                            dve.wait_ge(y_full, B * e + b + 1)
                            dve.tensor_scalar(ys[:, k, b], y_bank[b % 2][:, 0:D], gate_w[:, b, bass.ds(e, 1)], None, ALU.mult).then_inc(y_copied, 1)

                turns(dve, E // 2, turn_of_loop)
                dve.wait_ge(sum_in, 16)
                for b in range(B):
                    if b >= 2:
                        dve.wait_ge(out_ready, b - 1)
                    chain.link(dve.tensor_copy(half_b[:, b % 2], xn[:, TB * b:TB * (b + 1)]))
                    dve.tensor_tensor(x[:, TB * b:TB * (b + 1)], x[:, TB * b:TB * (b + 1)], half_b[:, b % 2], ALU.add).then_inc(out_ready, 1)


def setup(nc, ctx, dram):
    m = Memory()
    m.ctx = ctx
    m.x = ctx.enter_context(nc.sbuf_tensor("x_res", [P, NT, D], F32))
    m.ident = ctx.enter_context(nc.sbuf_tensor("ident", [P, P], F32))
    m.ps_max = ctx.enter_context(nc.psum_tensor("ps_max", [P, 2, 512], F32))
    m.ps_st = ctx.enter_context(nc.psum_tensor("ps_st", [P, 4, 512], F32))
    m.ps_out = ctx.enter_context(nc.psum_tensor("ps_out", [P, 512], F32))
    m.ps_misc = ctx.enter_context(nc.psum_tensor("ps_misc", [P, 512], F32))
    m.ident_in = ctx.enter_context(nc.semaphore("ident_in"))
    for name, shape in (("q_scr", (B, 2, D, T)), ("k_scr", (B, 2, D, T)), ("xs", ((SEL_TILES + 1) * P, D)),
                        ("ys", (SEL_TILES * P, D)), ("xl", (B * T, D)), ("acc", (B * T, D))):
        dram[name] = nc.dram_tensor(f"scratch_{name}", shape, F32).ap()
    return m, (lambda: attention(nc, m, 0, dram), lambda: moe_top1(nc, m, dram),
               lambda: attention(nc, m, 1, dram), lambda: moe_top_k(nc, m, dram))


def program(nc, dram):
    with ExitStack() as ctx:
        _, stages = setup(nc, ctx, dram)
        for stage in stages:
            stage()


def shape_constants(np):
    f = np.float32
    inv = (f(1.0) / (f(10000.0) ** (np.arange(0, HD, 2, dtype=f) / f(HD)))).astype(f)
    angle = np.outer(np.arange(T, dtype=f), inv).astype(f)
    angle = np.concatenate([angle, angle], axis=-1)
    cos, sin = np.cos(angle).astype(f), np.sin(angle).astype(f)
    sin[:, :HD // 2] *= -1
    per_q = lambda a: np.ascontiguousarray((a * f(HD ** -0.5)).reshape(TB, P, HD).transpose(1, 0, 2))

    def parts(a):
        bits = a.view(np.uint32)
        hi = ((bits + np.uint32(0x800)) & np.uint32(0xFFFFF000)).view(f)
        return hi, (a - hi).astype(f)

    slopes = np.array([2.0 ** (-8.0 * i / H) for i in range(1, H + 1)], dtype=f)
    bias = (slopes[:, None] * np.arange(T, dtype=f)[None]).reshape(NG, HG, T).astype(f)
    k_rows = np.zeros((2, NG, K_ROWS - BIAS_ROW, HG, T), f)
    q_rows = np.zeros((NG, MAX_ROW - BIAS_ROW, HG, T), f)
    hi, lo = parts(bias)
    k_rows[0, :, 0], k_rows[0, :, 1], k_rows[0, :, 2:4] = hi, lo, 1
    q_rows[:, 0:2] = 1
    hi, lo = parts(-bias)
    q_rows[:, 2], q_rows[:, 3] = hi, lo
    for h in range(HG):
        for part in range(2):
            k_rows[:, :, MAX_ROW - BIAS_ROW + HG * part + h, h] = 1
    e = np.arange(E)
    full = lambda a: np.ascontiguousarray(np.broadcast_to(a, (P, *a.shape)).astype(f))
    return {
        "cos_t": np.ascontiguousarray(np.tile(cos.T, (P // HD, 1))), "sin_t": np.ascontiguousarray(np.tile(sin.T, (P // HD, 1))),
        "cos_q": per_q(cos), "sin_q": per_q(sin),
        "ident": np.eye(P, dtype=f),
        "k_rows": k_rows.reshape(2 * NG, K_ROWS - BIAS_ROW, HG, T), "q_rows": q_rows,
        "upper": np.triu(np.ones((P, P), f), 1),
        "tie": full(f(E) - e.astype(f)),
        "steps": full(P * np.arange(NT, dtype=f)),
        "before": full((e[None] < e[:, None]).astype(f)),
        "tile_no": full(np.arange(SEL_TILES, dtype=f)),
        "row_base": (np.arange(B * E) // E * T).astype(f)[:, None],
    }


def laid_out(np, i):
    chunks = lambda w: np.ascontiguousarray(w.reshape(DC, P, -1).transpose(1, 0, 2))
    ctx = np.asarray(i["ctx_1024"])
    ctx_t = np.ascontiguousarray(ctx.transpose(0, 2, 1))
    swap = np.arange(D).reshape(H, 2, HD // 2)[:, ::-1].reshape(D)
    rep = lambda v: np.ascontiguousarray(np.broadcast_to(v, (P, v.shape[-1])))

    def experts(w1, w2):
        return (w1.reshape(E, DC, P, F).transpose(0, 2, 1, 3).reshape(E, P, DC * F),
                w2.reshape(E, FC, P, D).transpose(0, 2, 1, 3).reshape(E, P, FC * D))

    a1, a2 = experts(np.asarray(i["L0_ffn_W1"]), np.asarray(i["L0_ffn_W2"]))
    b1 = np.asarray(i["L0_ffn_b1"]).reshape(E, FC, P).transpose(0, 2, 1)
    b2 = np.broadcast_to(np.asarray(i["L0_ffn_b2"])[:, None], (E, P, D))
    return {
        "x": np.asarray(i["x"]), "ctx": ctx, "ctx_t": ctx_t, "ctx_r": np.ascontiguousarray(ctx_t[:, swap]),
        "rms_w": rep(np.asarray(i["L0_ffn_rms_w"])),
        "gate0": chunks(np.asarray(i["L0_ffn_gate_w"]).T),
        "w0": np.ascontiguousarray(np.concatenate([a1, a2, b1, b2], axis=2)),
        "wq": chunks(np.asarray(i["L1_xattn_Wq"]).T), "wk": chunks(np.asarray(i["L1_xattn_Wk"]).T),
        "wv": chunks(np.asarray(i["L1_xattn_Wv"]).T), "wo": chunks(np.asarray(i["L1_xattn_Wo"]).T),
        "bqk": np.ascontiguousarray(np.stack([np.asarray(i["L1_xattn_bq"]).reshape(DC, P).T, np.asarray(i["L1_xattn_bk"]).reshape(DC, P).T], axis=1)),
        "bv": rep(np.asarray(i["L1_xattn_bv"])), "bo": rep(np.asarray(i["L1_xattn_bo"])),
        "gate1": chunks(np.asarray(i["L1_ffn_gate_w"])),
        "w1": np.ascontiguousarray(np.concatenate(experts(np.asarray(i["L1_ffn_w1"]), np.asarray(i["L1_ffn_w2"])), axis=2)),
    }


def kernel(**inputs):
    import numpy as np
    import concourse.bacc as bacc
    from concourse import mybir as _mybir
    from concourse.bass_utils import run_bass_kernel_spmd as run

    nc = bacc.Bacc("TRN2", target_bir_lowering=False, num_devices=1)
    arrays, dram = {}, {}
    for name, a in {**laid_out(np, inputs), **shape_constants(np)}.items():
        arrays[f"in_{name}"] = a
        dram[name] = nc.dram_tensor(f"in_{name}", a.shape, _mybir.dt.from_np(a.dtype), kind="ExternalInput").ap()
    dram["out"] = nc.dram_tensor("out_x", (B, T, D), F32, kind="ExternalOutput").ap()
    program(nc, dram)
    return run(nc, [arrays], core_ids=[0]).results[0]["out_x"]
```

```python
from contextlib import ExitStack

import concourse.bass as bass
from concourse import mybir

ALU = mybir.AluOpType
ACT = mybir.ActivationFunctionType
AX = mybir.AxisListType
F32 = mybir.dt.float32
F32R = mybir.dt.float32r
BF16 = mybir.dt.bfloat16
I32 = mybir.dt.int32
U32 = mybir.dt.uint32

P = 128
B, T, D = 4, 512, 256
H, HD = 16, 16
E, F = 8, 1024
NT = B * T // P
TB = T // P
DC = D // P
FC = F // P
HG = 4
NG = H // HG
SLOTS = B * NG
STEPS = SLOTS * TB
VW = 32
BIAS_ROW = 3 * HD
MAX_ROW = 96
MAX_ROWS = 2 * HG
BIAS_ROWS = 4
K_ROWS = MAX_ROW + MAX_ROWS
SEL_TILES = B * T // P + E
ROW = D + 1
CAP = 2 * T // E
LN_EPS = 1e-5
RMS_EPS = 1e-6
RSQRT_MAGIC = float(0x5F3759DF)
W0_COLS = DC * F + FC * D + FC + D


class Counter:

    def __init__(self, eng, sem):
        self.eng, self.sem, self.n = eng, sem, 0

    def link(self, ins):
        self.n += 1
        ins.then_inc(self.sem, 1)
        self.eng.wait_ge(self.sem, self.n)


def wait_from(eng, sem, value):
    if not isinstance(value, int) or value > 0:
        eng.wait_ge(sem, value)


def turns(eng, n, body):
    body(0)
    with eng.Fori(1, n) as it:
        body(it)


def rsqrt(dve, chain, y, x, tmp, scale, eps):
    v, u = tmp
    chain.link(dve.tensor_scalar(v, x, scale, eps, ALU.mult, ALU.add))
    chain.link(dve.tensor_scalar(u.bitcast(I32), v.bitcast(I32), 1, None, ALU.logical_shift_right))
    chain.link(dve.tensor_scalar(y.bitcast(I32), u.bitcast(I32), -1.0, RSQRT_MAGIC, ALU.mult, ALU.add))
    for _ in range(4):
        chain.link(dve.tensor_tensor(u, y, y, ALU.mult))
        chain.link(dve.scalar_tensor_tensor(u, u, -0.5, v, ALU.mult, ALU.mult))
        chain.link(dve.scalar_tensor_tensor(y, u, 1.5, y, ALU.add, ALU.mult))


class Memory:
    pass


def attention_schedule(layer):
    jobs = {t: [] for t in range(-9, STEPS + 8)}
    qkinds = ["q"] if layer == 0 else ["qt", "q"]
    if layer == 1:
        jobs[-9] += [("k", 0, 0), ("k", 0, 1), ("v", 0, 0), ("v", 0, 1)]
    jobs[-9] += [(kind, i) for i in range(TB) for kind in qkinds]
    for s in range(SLOTS):
        jobs[4 * s - 4].append(("m", s))
        jobs[4 * s + 5].append(("o", s))
    for b in range(1, B):
        if layer == 0:
            for j, dt in enumerate((-18, -17, -14, -13)):
                jobs[16 * b + dt].append(("q", TB * b + j))
            continue
        t0, ks, qts, qs = (-8, (0, 1), (1, 2, 3, 5), (2, 3, 4, 6)) if b == 1 else (16 * b - 32, (2, 6), (1, 5, 8, 12), (3, 7, 9, 13))
        for half in range(2):
            jobs[t0 + ks[half]].append(("k", b, half))
        for j in range(TB):
            jobs[t0 + qs[j]].append(("q", TB * b + j))
            jobs[t0 + qts[j]].append(("qt", TB * b + j))
        jobs[16 * b - 6].append(("v", b, 0))
        jobs[16 * b - 5].append(("v", b, 1))
    if layer == 1:
        for b in range(B):
            at0, at1, a0, a1 = (19, 23, 30, 31) if b < B - 1 else (18, 18, 19, 19)
            jobs[16 * b + at0].append(("at", b, 0))
            jobs[16 * b + at1].append(("at", b, 1))
            jobs[16 * b + a0].append(("a", b, 0))
            jobs[16 * b + a1].append(("a", b, 1))
    index, n = {}, 0
    for t in sorted(jobs):
        for job in jobs[t]:
            index[job] = n
            n += 1
    return jobs, index


def attention(nc, m, layer, dram):
    jobs, index = attention_schedule(layer)
    LT = sorted(jobs)
    keys_at = {b: max(16 * b - 24, -4) for b in range(1, B)} if layer == 0 else {j[1]: t for t in LT for j in jobs[t] if j[0] == "k"}
    tile_at = {j[1]: t for t in LT for j in jobs[t] if j[0] == ("q" if layer == 0 else "qt")}
    with ExitStack() as ctx:
        def sb(name, shape, dt):
            return ctx.enter_context(nc.sbuf_tensor(f"a{layer}_{name}", shape, dt))

        def sem(name):
            return m.ctx.enter_context(nc.semaphore(f"a{layer}_{name}"))

        ka = sb("ka", [P, NG, HG, T], F32R)
        qa = sb("qa", [P, NG, HG, T], F32R)
        probs = sb("probs", [P, 3, HG, T], F32)
        vaug = sb("vaug", [P, 2, TB, H, VW], F32)
        ctx_t = sb("ctx_t", [P, 2, DC, T], F32)
        kf = sb("kf", [P, DC, T], F32)
        kst = sb("kst", [P, 2, DC, T], F32R)
        qst = sb("qst", [P, 2, 2, DC, P], F32R)
        xn = sb("xn", [P, 2, D], F32)
        neg_max = sb("neg_max", [P, 2, TB, 2, HG], F32R)
        row_max = sb("row_max", [P, 3, HG, TB], F32)
        max_t = sb("max_t", [MAX_ROWS, 2, T], F32R)
        out_sb = sb("out_sb", [P, T], F32)
        rden = sb("rden", [P, TB, HG], F32)
        stats = sb("stats", [P, NT, 6], F32)
        mv = sb("mv", [P, NT, 2], F32)
        rstd = sb("rstd", [P, NT], F32)
        neg_mean = sb("neg_mean", [P, NT], F32)
        tmp = [sb(f"tmp{i}", [P, NT], F32) for i in range(2)]
        if layer == 0:
            ctx_r = sb("ctx_r", [P, 2, DC, T], F32)
            ctx_v = sb("ctx_v", [P, 2, TB, D], F32)
            kf2 = sb("kf2", [P, DC, T], F32)
            cos_t = sb("cos_t", [P, T], F32)
            sin_t = sb("sin_t", [P, T], F32)
            cos_q = sb("cos_q", [P, TB, HD], F32)
            sin_q = sb("sin_q", [P, TB, HD], F32)
            rope_a = sb("rope_a", [P, D], F32)
            rope_b = sb("rope_b", [P, D], F32)
            att = sb("att", [P, 2, TB, HG * HD], F32)
        else:
            wq, wk, wv, wo = (sb(f"w{c}", [P, DC, D], F32) for c in "qkvo")
            bqk = sb("bqk", [P, 2, DC], F32)
            bv = sb("bv", [P, D], F32)
            bo = sb("bo", [P, D], F32)
            xnt = sb("xnt", [P, 2, DC, P], F32)
            qf = sb("qf", [P, 2, DC, P], F32)
            att = sb("att", [P, 2, TB, D], F32)
            att_t = sb("att_t", [P, DC, T], F32)

        x_in = [sem(f"x_in{b}") for b in range(B)] if layer == 0 else []
        consts_in = sem("consts_in")
        zero_set = sem("zero_set")
        rows_in = sem("rows_in")
        vaug_set = sem("vaug_set")
        ctx_in = [sem(f"ctx_in{i}") for i in range(2)]
        ctx_used = sem("ctx_used")
        k_ready = sem("k_ready")
        k_stored = sem("k_stored")
        q_ready = sem("q_ready")
        q_stored = [sem(f"q_stored{i}") for i in range(2)]
        loaded = [sem(f"loaded{i}") for i in range(NG)]
        stats_done = sem("stats_done")
        normed_done = sem("normed_done")
        xn_ready = sem("xn_ready")
        misc_full = sem("misc_full")
        misc_free = sem("misc_free")
        mx_full = sem("mx_full")
        mx_read = sem("mx_read")
        neg_ready = sem("neg_ready")
        max_in = [sem(f"max_in{i}") for i in range(NG)]
        st_full = sem("st_full")
        exp_done = sem("exp_done")
        v_ready = sem("v_ready")
        pv_done = sem("pv_done")
        out_copied = sem("out_copied")
        att_added = sem("att_added")
        dve_chain = sem("dve_chain")
        pool_chain = sem("pool_chain")

        x = m.x
        misc = m.ps_misc
        n_const = 4 if layer == 0 else 7
        n_ctx = 3 if layer == 0 else 1
        n_rows = 3 if layer == 0 else 1
        norm_kind = "q" if layer == 0 else "qt"
        k_scr = dram["k_scr"]
        q_scr = dram["q_scr"]

        with nc.Block() as block:

            @block.sync
            def _(sp):
                def load_ctx(b):
                    if b >= B:
                        return
                    if b >= 2:
                        sp.wait_ge(ctx_used, b - 1)
                    sp.dma_start(ctx_t[:, b % 2], dram["ctx_t"][b].rearrange("(c p) t -> p c t", p=P)).then_inc(ctx_in[b % 2], 16)
                    if layer == 0:
                        sp.dma_start(ctx_r[:, b % 2], dram["ctx_r"][b].rearrange("(c p) t -> p c t", p=P)).then_inc(ctx_in[b % 2], 16)
                        sp.dma_start(ctx_v[:, b % 2], dram["ctx"][b].rearrange("(j p) d -> p j d", p=P)).then_inc(ctx_in[b % 2], 16)

                def store_k(b):
                    sp.wait_ge(k_ready, b + 1)
                    for part in range(2):
                        sp.dma_start(k_scr[b, part].rearrange("(c p) t -> p c t", p=P), kst[:, part].bitcast(F32)).then_inc(k_stored, 16)

                def store_q(i):
                    b, j = i // TB, i % TB
                    sp.wait_ge(q_ready, i + 1)
                    for part in range(2):
                        sp.dma_start(q_scr[b, part, :, j * P:(j + 1) * P].rearrange("(c p) t -> p c t", p=P),
                                     qst[:, i % 2, part].bitcast(F32)).then_inc(q_stored[i % 2], 16)

                def load_group(b, g):
                    s = NG * b + g
                    if g == 0:
                        sp.wait_ge(zero_set, 2)
                        sp.wait_ge(k_stored, 32 * (b + 1))
                        for i in range(2):
                            sp.wait_ge(q_stored[i], 32 * (TB // 2) * (b + 1))
                    if b >= 1:
                        sp.wait_ge(st_full, 8 * (s - NG + 1))
                    rows = slice(g * HG * HD, (g + 1) * HG * HD)
                    for r, (qpart, kpart) in enumerate(((0, 0), (1, 0), (0, 1))):
                        sp.dma_start(qa[HD * r:HD * (r + 1), g].bitcast(F32), q_scr[b, qpart, rows].rearrange("(h d) t -> d h t", d=HD)).then_inc(loaded[g], 16)
                        sp.dma_start(ka[HD * r:HD * (r + 1), g].bitcast(F32), k_scr[b, kpart, rows].rearrange("(h d) t -> d h t", d=HD)).then_inc(loaded[g], 16)

                if layer == 0:
                    sp.dma_start(x[:, 0:TB], dram["x"][0].rearrange("(j p) d -> p j d", p=P)).then_inc(x_in[0], 16)
                    for dst, src in ((cos_t, "cos_t"), (sin_t, "sin_t"), (cos_q, "cos_q"), (sin_q, "sin_q")):
                        sp.dma_start(dst[:], dram[src]).then_inc(consts_in, 16)
                load_ctx(0)
                if layer == 0:
                    sp.dma_start(m.ident[:], dram["ident"]).then_inc(m.ident_in, 16)
                    for b in range(1, B):
                        sp.dma_start(x[:, TB * b:TB * (b + 1)], dram["x"][b].rearrange("(j p) d -> p j d", p=P)).then_inc(x_in[b], 16)
                else:
                    for dst, src in ((wq, "wq"), (wk, "wk"), (wv, "wv"), (wo, "wo"), (bqk, "bqk"), (bv, "bv"), (bo, "bo")):
                        sp.dma_start(dst[:], dram[src]).then_inc(consts_in, 16)
                load_ctx(1)
                store_k(0)
                for i in range(TB):
                    store_q(i)
                for g in range(NG):
                    load_group(0, g)
                load_ctx(2)
                for t in LT[1:]:
                    for b in range(1, B):
                        if t == (16 * b - 18 if layer == 0 else keys_at[b] + 1):
                            store_k(b)
                        if t == 16 * b - 4:
                            load_ctx(b + 2)
                    for job in jobs[t]:
                        if job[0] == "q":
                            store_q(job[1])
                    for b in range(1, B):
                        for g in range(NG):
                            if t == 16 * b - 12 + 4 * g:
                                load_group(b, g)

            @block.gpsimd
            def _(pool):
                chain = Counter(pool, pool_chain)
                for g in range(NG):
                    ins = pool.memset(qa[:, g].bitcast(F32), 0.0)
                ins.then_inc(zero_set, 1)

                pool.wait_ge(zero_set, 2)
                pool.dma_start(ka[MAX_ROW:K_ROWS], dram["k_select"]).then_inc(rows_in, 16)
                if layer == 0:
                    pool.dma_start(ka[BIAS_ROW:BIAS_ROW + BIAS_ROWS], dram["k_bias"]).then_inc(rows_in, 16)
                    pool.dma_start(qa[BIAS_ROW:BIAS_ROW + BIAS_ROWS], dram["q_bias"]).then_inc(rows_in, 16)

                def keys(b):
                    if layer == 0:
                        pool.wait_ge(k_stored, 32 * b)
                        pool.wait_ge(ctx_in[b % 2], 16 * n_ctx * (b // 2 + 1))
                        pool.tensor_tensor(kf[:], ctx_t[:, b % 2], cos_t[:].unsqueeze(1).to_broadcast([P, DC, T]), ALU.mult)
                        chain.link(pool.tensor_tensor(kf2[:], ctx_r[:, b % 2], sin_t[:].unsqueeze(1).to_broadcast([P, DC, T]), ALU.mult))
                        chain.link(pool.tensor_tensor(kf[:], kf[:], kf2[:], ALU.add))
                        chain.link(pool.tensor_copy(kst[:, 0], kf[:]))
                    else:
                        pool.wait_ge(misc_free, index["k", b, 1] + 1)
                    pool.tensor_tensor(kst[:, 1], kf[:], kst[:, 0].bitcast(F32), ALU.subtract).then_inc(k_ready, 1)

                def values(b):
                    if b >= 2:
                        pool.wait_ge(pv_done, 16 * (b - 1))
                    else:
                        pool.wait_ge(vaug_set, 2)
                        pool.wait_ge(ctx_in[b % 2], 16 * n_ctx)
                    pool.tensor_copy(vaug[:, b % 2, :, :, 0:HD], ctx_v[:, b % 2].rearrange("p j (h d) -> p j h d", d=HD)).then_inc(v_ready, 1)
                    pool.wait_ge(v_ready, b + 1)
                    pool.engine_nop().then_inc(ctx_used, 1)

                def rotated(i):
                    j = i % TB
                    pool.wait_ge(normed_done, i + 1)
                    if i:
                        pool.wait_ge(xn_ready, i)
                    xh = xn[:, i % 2].rearrange("p (h d) -> p h d", d=HD)
                    ah = rope_a[:].rearrange("p (h d) -> p h d", d=HD)
                    bh = rope_b[:].rearrange("p (h d) -> p h d", d=HD)
                    cb = cos_q[:, j].unsqueeze(1).to_broadcast([P, H, HD])
                    half = HD // 2
                    pool.tensor_tensor(ah, xh, cb, ALU.mult)
                    pool.tensor_tensor(bh[:, :, 0:half], xh[:, :, half:HD], sin_q[:, j, 0:half].unsqueeze(1).to_broadcast([P, H, half]), ALU.mult)
                    chain.link(pool.tensor_tensor(bh[:, :, half:HD], xh[:, :, 0:half], sin_q[:, j, half:HD].unsqueeze(1).to_broadcast([P, H, half]), ALU.mult))
                    pool.tensor_tensor(xn[:, i % 2], rope_a[:], rope_b[:], ALU.add).then_inc(xn_ready, 1)

                def split_q(i):
                    pool.wait_ge(misc_free, index["q", i] + 1)
                    if i >= 2:
                        pool.wait_ge(q_stored[i % 2], 32 * (i // 2))
                    pool.tensor_tensor(qst[:, i % 2, 1], qf[:, i % 2], qst[:, i % 2, 0].bitcast(F32), ALU.subtract).then_inc(q_ready, 1)

                if layer == 0:
                    pool.wait_ge(consts_in, 16 * n_const)
                    for i in range(TB):
                        rotated(i)
                    values(0)
                else:
                    keys(0)
                    for i in range(TB):
                        split_q(i)
                for t in LT[1:]:
                    for b in range(1, B):
                        if t == keys_at[b]:
                            keys(b)
                        if layer == 0 and t == 16 * b - 12:
                            values(b)
                    for job in jobs.get(t + 2, []):
                        if job[0] == "q" and layer == 0:
                            rotated(job[1])
                    for job in jobs[t]:
                        if job[0] == "q" and layer == 1:
                            split_q(job[1])
                        if job[0] == "o" and layer == 0:
                            s = job[1]
                            b, g = s // NG, s % NG
                            pool.wait_ge(misc_free, index[job] + 1)
                            xs = x[:, TB * b:TB * (b + 1), g * HG * HD:(g + 1) * HG * HD]
                            pool.tensor_tensor(xs, xs, att[:, s % 2], ALU.add).then_inc(att_added, 1)
                        if job[0] == "a" and job[2] == 1:
                            b = job[1]
                            pool.wait_ge(misc_free, index[job] + 1)
                            xs = x[:, TB * b:TB * (b + 1)]
                            pool.tensor_tensor(xs, xs, bo[:].unsqueeze(1).to_broadcast([P, TB, D]), ALU.add).then_inc(att_added, 1)

            @block.tensor
            def _(pe):
                def fill(job):
                    if index[job]:
                        pe.wait_ge(misc_free, index[job])

                def job_m(job):
                    s = job[1]
                    pe.wait_ge(neg_ready, s + 1)
                    fill(job)
                    for qt in range(TB):
                        ins = pe.transpose(misc[0:MAX_ROWS, qt * P:(qt + 1) * P],
                                           neg_max[:, s % 2, qt].rearrange("p a h -> p (a h)").bitcast(F32), m.ident[:])
                    ins.then_inc(misc_full, 1)

                def job_o(job):
                    pe.wait_ge(out_copied, job[1] + 1)
                    fill(job)
                    for qt in range(TB):
                        ins = pe.transpose(misc[:, qt * P:(qt + 1) * P], out_sb[:, qt * P:(qt + 1) * P], m.ident[:])
                    ins.then_inc(misc_full, 1)

                def job_xt(job):
                    i = job[1]
                    pe.wait_ge(xn_ready, i + 1)
                    fill(job)
                    for c in range(DC):
                        ins = pe.transpose(misc[:, c * P:(c + 1) * P], xn[:, i % 2, c * P:(c + 1) * P], m.ident[:])
                    ins.then_inc(misc_full, 1)

                def job_q1(job):
                    i = job[1]
                    fill(job)
                    for o in range(DC):
                        for c in range(DC):
                            ins = pe.matmul(misc[:, o * P:(o + 1) * P], wq[:, c, o * P:(o + 1) * P], xnt[:, i % 2, c], start=(c == 0), stop=(c == DC - 1))
                    ins.then_inc(misc_full, 1)

                def job_k(job):
                    _, b, o = job
                    pe.wait_ge(ctx_in[b % 2], 16 * n_ctx * (b // 2 + 1))
                    fill(job)
                    for c in range(DC):
                        ins = pe.matmul(misc[:], wk[:, c, o * P:(o + 1) * P], ctx_t[:, b % 2, c], start=(c == 0), stop=(c == DC - 1))
                    ins.then_inc(misc_full, 1)

                def job_v(job):
                    _, b, half = job
                    fill(job)
                    for jj in range(2):
                        j = 2 * half + jj
                        for c in range(DC):
                            ins = pe.matmul(misc[:, jj * D:(jj + 1) * D], ctx_t[:, b % 2, c, j * P:(j + 1) * P], wv[:, c], start=(c == 0), stop=(c == DC - 1))
                    ins.then_inc(misc_full, 1)

                def job_at(job):
                    _, b, c = job
                    fill(job)
                    for qt in range(TB):
                        ins = pe.transpose(misc[:, qt * P:(qt + 1) * P], att[:, b % 2, qt, c * P:(c + 1) * P], m.ident[:])
                    ins.then_inc(misc_full, 1)

                def job_a(job):
                    _, b, half = job
                    fill(job)
                    for jj in range(2):
                        qt = 2 * half + jj
                        for c in range(DC):
                            ins = pe.matmul(misc[:, jj * D:(jj + 1) * D], att_t[:, c, qt * P:(qt + 1) * P], wo[:, c], start=(c == 0), stop=(c == DC - 1))
                    ins.then_inc(misc_full, 1)

                run = {"m": job_m, "o": job_o, "k": job_k, "v": job_v, "at": job_at, "a": job_a,
                       "q": job_xt if layer == 0 else job_q1, "qt": job_xt}

                def maxima_scores(u, qt):
                    if not 0 <= u < STEPS:
                        return
                    s, h = u // HG, u % HG
                    b, g = s // NG, s % NG
                    if h == 0 and qt == 0:
                        pe.wait_ge(loaded[g], 96 * (b + 1))
                    n = TB * u + qt
                    if n >= 2:
                        pe.wait_ge(mx_read, n - 1)
                    pe.matmul(m.ps_max[:, n % 2], qa[0:MAX_ROW, g, h, qt * P:(qt + 1) * P], ka[0:MAX_ROW, g, h],
                              start=True, stop=True).then_inc(mx_full, 1)

                def scores(t, pair):
                    if not 0 <= t < STEPS:
                        return
                    s, kc = t // TB, t % TB
                    b, g = s // NG, s % NG
                    if kc == 0 and pair == 0:
                        pe.wait_ge(max_in[g], 16 * (b + 1))
                    n = 2 * t + pair
                    if n >= 2:
                        pe.wait_ge(exp_done, n - 1)
                    for hh in range(2):
                        h = 2 * pair + hh
                        ins = pe.matmul(m.ps_st[:, 2 * (n % 2) + hh], ka[0:K_ROWS, g, h, kc * P:(kc + 1) * P], qa[0:K_ROWS, g, h],
                                        start=True, stop=True)
                    ins.then_inc(st_full, 1)

                def weigh(t):
                    s, kc = t // TB, t % TB
                    b, g = s // NG, s % NG
                    pe.wait_ge(exp_done, 2 * t + 2)
                    if kc == 0:
                        pe.wait_ge(v_ready, (b + 1) if layer == 0 else 2 * (b + 1))
                        if s:
                            pe.wait_ge(out_copied, s)
                    for h in range(HG):
                        ins = pe.matmul(m.ps_out[VW * h:VW * (h + 1)], vaug[:, b % 2, kc, HG * g + h], probs[:, t % 3, h],
                                        start=(kc == 0), stop=(kc == TB - 1))
                    ins.then_inc(pv_done, 1)

                pe.wait_ge(m.ident_in, 16)
                if layer == 1:
                    pe.wait_ge(consts_in, 16 * n_const)
                for job in jobs[LT[0]]:
                    run[job[0]](job)
                pe.wait_ge(rows_in, 16 * n_rows)
                for t in LT[1:]:
                    scores(t, 0)
                    maxima_scores(t + 8, 0)
                    scores(t, 1)
                    maxima_scores(t + 8, 1)
                    if 0 <= t - 1 < STEPS:
                        weigh(t - 1)
                    for job in jobs[t][:-1]:
                        run[job[0]](job)
                    maxima_scores(t + 8, 2)
                    maxima_scores(t + 8, 3)
                    for job in jobs[t][-1:]:
                        run[job[0]](job)

            @block.scalar
            def _(act):
                def take(job):
                    act.wait_ge(misc_full, index[job] + 1)

                def act_job(job):
                    if job[0] == "m":
                        s = job[1]
                        b, g = s // NG, s % NG
                        if s >= 2:
                            act.wait_ge(max_in[(s - 2) % NG], 16 * ((s - 2) // NG + 1))
                        take(job)
                        nc.scalar.copy(max_t[:, s % 2], misc[0:MAX_ROWS]).then_inc(misc_free, 1)
                        act.wait_ge(misc_free, index[job] + 1)
                        if b >= 1:
                            act.wait_ge(st_full, 8 * (s - NG + 1))
                        act.dma_start(qa[MAX_ROW:K_ROWS, g].bitcast(F32),
                                      max_t[:, s % 2].bitcast(F32).unsqueeze(1).to_broadcast([MAX_ROWS, HG, T])).then_inc(max_in[g], 16)
                    elif job[0] == "qt":
                        take(job)
                        nc.scalar.copy(xnt[:, job[1] % 2], misc[:, 0:D].rearrange("p (c t) -> p c t", c=DC)).then_inc(misc_free, 1)
                    elif job[0] == "k":
                        _, b, o = job
                        if b >= 1:
                            act.wait_ge(k_ready, b)
                            act.wait_ge(k_stored, 32 * b)
                        take(job)
                        nc.scalar.activation(kf[:, o], misc[:], ACT.Identity, bias=bqk[:, 1, o:o + 1])
                        nc.scalar.activation(kst[:, 0, o], misc[:], ACT.Identity, bias=bqk[:, 1, o:o + 1]).then_inc(misc_free, 1)
                    elif job[0] == "at":
                        _, b, c = job
                        take(job)
                        nc.scalar.copy(att_t[:, c], misc[:]).then_inc(misc_free, 1)

                def normed(i):
                    act.wait_ge(stats_done, 1 if i < TB else 2)
                    if i >= 2:
                        act.wait_ge(misc_full, index[norm_kind, i - 2] + 1)
                    nc.scalar.activation(xn[:, i % 2], x[:, i], ACT.Identity, bias=neg_mean[:, i:i + 1],
                                         scale=rstd[:, i:i + 1]).then_inc(normed_done if layer == 0 else xn_ready, 1)

                if layer == 1:
                    act.wait_ge(consts_in, 16 * n_const)
                for job in jobs[LT[0]]:
                    if job == (norm_kind, 0):
                        normed(0)
                        normed(1)
                    act_job(job)
                    if job[0] == norm_kind and job[1] + 2 < TB:
                        normed(job[1] + 2)
                act.wait_ge(rows_in, 16 * n_rows)
                for t in LT[1:]:
                    if 0 <= t < STEPS:
                        for pair in range(2):
                            n = 2 * t + pair
                            act.wait_ge(st_full, n + 1)
                            if t >= 3:
                                act.wait_ge(pv_done, t - 2)
                            nc.scalar.activation(probs[:, t % 3, 2 * pair:2 * pair + 2], m.ps_st[:, 2 * (n % 2):2 * (n % 2) + 2], ACT.Exp).then_inc(exp_done, 1)
                    if t >= TB and t % TB == 0 and t // TB <= SLOTS:
                        s = t // TB - 1
                        if s:
                            act.wait_ge(misc_full, index["o", s - 1] + 1)
                        act.wait_ge(pv_done, TB * (s + 1))
                        nc.scalar.copy(out_sb[:], m.ps_out[:]).then_inc(out_copied, 1)
                    for job in jobs[t]:
                        act_job(job)
                    for i in range(NT):
                        if tile_at[i] == t + 2 or (t == LT[1] < tile_at[i] < t + 2):
                            normed(i)

            @block.vector
            def _(dve):
                chain = Counter(dve, dve_chain)

                def take(job):
                    dve.wait_ge(misc_full, index[job] + 1)

                def tile_stats(b0, b1):
                    if layer == 0:
                        for b in range(b0, b1):
                            dve.wait_ge(x_in[b], 16)
                    tiles = range(TB * b0, TB * b1)
                    cols = slice(TB * b0, TB * b1)
                    for i in tiles:
                        ins = dve.bn_stats(stats[:, i], x[:, i])
                    chain.link(ins)
                    for i in tiles:
                        ins = dve.bn_aggr(mv[:, i], stats[:, i])
                    chain.link(ins)
                    rsqrt(dve, chain, rstd[:, cols], mv[:, cols, 1], [z[:, cols] for z in tmp], 1.0, LN_EPS)
                    dve.scalar_tensor_tensor(neg_mean[:, cols], mv[:, cols, 0], -1.0, rstd[:, cols], ALU.mult, ALU.mult).then_inc(stats_done, 1)

                def first_keys():
                    dve.wait_ge(consts_in, 16 * n_const)
                    dve.wait_ge(ctx_in[0], 16 * n_ctx)
                    dve.tensor_tensor(kf[:], ctx_t[:, 0], cos_t[:].unsqueeze(1).to_broadcast([P, DC, T]), ALU.mult)
                    chain.link(dve.tensor_tensor(kf2[:], ctx_r[:, 0], sin_t[:].unsqueeze(1).to_broadcast([P, DC, T]), ALU.mult))
                    chain.link(dve.tensor_tensor(kf[:], kf[:], kf2[:], ALU.add))
                    chain.link(dve.tensor_copy(kst[:, 0], kf[:]))
                    dve.tensor_tensor(kst[:, 1], kf[:], kst[:, 0].bitcast(F32), ALU.subtract).then_inc(k_ready, 1)

                def dve_job(job):
                    if job[0] == "q" and layer == 0:
                        i = job[1]
                        if i >= 2:
                            dve.wait_ge(q_stored[i % 2], 32 * (i // 2))
                        take(job)
                        src = misc[:, 0:D].rearrange("p (c t) -> p c t", c=DC)
                        chain.link(dve.tensor_copy(qst[:, i % 2, 0], src))
                        chain.link(dve.tensor_tensor(qst[:, i % 2, 1], src, qst[:, i % 2, 0].bitcast(F32), ALU.subtract))
                        dve.engine_nop().then_inc(misc_free, 1)
                        dve.engine_nop().then_inc(q_ready, 1)
                    elif job[0] == "q":
                        i = job[1]
                        if i >= 2:
                            dve.wait_ge(q_ready, i - 1)
                            dve.wait_ge(q_stored[i % 2], 32 * (i // 2))
                        take(job)
                        for dst in (qf[:, i % 2], qst[:, i % 2, 0]):
                            for o in range(DC):
                                ins = dve.tensor_scalar(dst[:, o], misc[:, o * P:(o + 1) * P], bqk[:, 0, o:o + 1], HD ** -0.5, ALU.add, ALU.mult)
                        ins.then_inc(misc_free, 1)
                    elif job[0] == "v":
                        _, b, half = job
                        if b >= 2:
                            dve.wait_ge(pv_done, 16 * (b - 1))
                        take(job)
                        chain.link(dve.tensor_tensor(
                            vaug[:, b % 2, 2 * half:2 * half + 2, :, 0:HD],
                            misc[:].rearrange("p (j h d) -> p j h d", j=2, d=HD),
                            bv[:].rearrange("p (h d) -> p h d", d=HD).unsqueeze(1).to_broadcast([P, 2, H, HD]), ALU.add))
                        dve.engine_nop().then_inc(misc_free, 1)
                        dve.engine_nop().then_inc(v_ready, 1)
                        if half == 1:
                            dve.engine_nop().then_inc(ctx_used, 1)
                    elif job[0] == "o":
                        s = job[1]
                        b, g = s // NG, s % NG
                        take(job)
                        o = misc[:].rearrange("p (j h w) -> p j h w", j=TB, w=VW)
                        chain.link(dve.reciprocal(rden[:], o[:, :, :, HD]))
                        if layer == 0:
                            dst = att[:, s % 2].rearrange("p j (h d) -> p j h d", d=HD)
                            if s >= 2:
                                dve.wait_ge(att_added, s - 1)
                        else:
                            dst = att[:, b % 2, :, g * HG * HD:(g + 1) * HG * HD].rearrange("p j (h d) -> p j h d", d=HD)
                        dve.tensor_tensor(dst, o[:, :, :, 0:HD], rden[:].unsqueeze(3).to_broadcast([P, TB, HG, HD]), ALU.mult).then_inc(misc_free, 1)
                    elif job[0] == "a":
                        _, b, half = job
                        take(job)
                        xs = x[:, TB * b + 2 * half:TB * b + 2 * half + 2]
                        dve.tensor_tensor(xs, misc[:].rearrange("p (j d) -> p j d", j=2), xs, ALU.add).then_inc(misc_free, 1)

                def maxima(u, qt):
                    if not 0 <= u < STEPS:
                        return
                    s, h = u // HG, u % HG
                    n = TB * u + qt
                    dve.wait_ge(mx_full, n + 1)
                    dve.tensor_reduce(row_max[:, s % 3, h, qt:qt + 1], m.ps_max[:, n % 2], AX.X, ALU.max).then_inc(mx_read, 1)
                    if h == HG - 1 and qt == TB - 1:
                        dve.wait_ge(mx_read, TB * (u + 1))
                        if s >= 2:
                            dve.wait_ge(misc_full, index["m", s - 2] + 1)
                        src = row_max[:, s % 3].rearrange("p h j -> p j h")
                        chain.link(dve.tensor_scalar(neg_max[:, s % 2, :, 0], src, -1.0, None, ALU.mult))
                        dve.scalar_tensor_tensor(neg_max[:, s % 2, :, 1], src, -1.0, neg_max[:, s % 2, :, 0].bitcast(F32),
                                                 ALU.mult, ALU.subtract).then_inc(neg_ready, 1)

                def clear_keys():
                    for g in range(NG):
                        ins = dve.memset(ka[:, g].bitcast(F32), 0.0)
                    ins.then_inc(zero_set, 1)

                if layer == 0:
                    clear_keys()
                tile_stats(0, 1)
                if layer == 0:
                    first_keys()
                else:
                    clear_keys()
                dve.memset(vaug[:, :, :, :, HD:HD + 1], 1.0).then_inc(vaug_set, 1)
                dve.memset(vaug[:, :, :, :, HD + 1:VW], 0.0).then_inc(vaug_set, 1)
                if layer == 1:
                    dve.wait_ge(consts_in, 16 * n_const)
                for job in jobs[LT[0]]:
                    dve_job(job)
                tile_stats(1, B)
                for t in LT[1:]:
                    for qt in range(TB):
                        maxima(t + 8, qt)
                        for job in (jobs[t][:-1] if qt == 1 else jobs[t][-1:] if qt == 3 else []):
                            dve_job(job)


def moe_top1(nc, m, dram):
    with ExitStack() as ctx:
        def sb(name, shape, dt):
            return ctx.enter_context(nc.sbuf_tensor(f"e0_{name}", shape, dt))

        def sem(name):
            return m.ctx.enter_context(nc.semaphore(f"e0_{name}"))

        x = m.x
        xn = sb("xn", [P, NT, ROW], F32)
        xnt = sb("xnt", [P, 2, 2, DC, P], F32)
        rms_w = sb("rms_w", [P, D], F32)
        gate = sb("gate", [P, DC, E], F32)
        upper = sb("upper", [P, P], F32)
        tie = sb("tie", [P, E], F32)
        steps = sb("steps", [P, NT], F32)
        before = sb("before", [P, E, E], F32)
        tile_no = sb("tile_no", [P, SEL_TILES], F32)
        upper_b = sb("upper_b", [P, P], BF16)
        ones_b = sb("ones_b", [P, P], BF16)
        pad = sb("pad", [P, SEL_TILES + 1, ROW], F32)
        number = sb("number", [P, NT + SEL_TILES + 1], U32)
        stats = sb("stats", [P, NT, 6], F32)
        mv = sb("mv", [P, NT, 2], F32)
        rstd = sb("rstd", [P, NT], F32)
        neg_mean = sb("neg_mean", [P, NT], F32)
        tmp = [sb(f"tmp{i}", [P, NT], F32) for i in range(2)]
        logits = sb("logits", [P, NT, E], F32)
        prob = sb("prob", [P, NT, E], F32)
        work = sb("work", [P, NT, E], F32)
        top = sb("top", [P, NT], F32)
        score = sb("score", [P, NT], F32)
        onehot = sb("onehot", [P, NT, E], F32)
        onehot_b = sb("onehot_b", [P, NT, E], BF16)
        count = sb("count", [P, E], F32)
        tiles_e = sb("tiles_e", [P, E], F32)
        base = sb("base", [P, E], F32)
        last = sb("last", [P, E], F32)
        cmp = sb("cmp", [P, E, NT], F32)
        pre = sb("pre", [P, E, E], F32)
        which = sb("which", [P, SEL_TILES, E], F32)
        expert_f = sb("expert_f", [P, SEL_TILES], F32)
        expert = sb("expert", [P, SEL_TILES], I32)
        slot_f = sb("slot_f", [P, NT], F32)
        slot = sb("slot", [P, NT], U32)
        wts = sb("wts", [P, 2, W0_COLS], F32)
        xs = sb("xs", [P, 2, ROW], F32)
        xst = sb("xst", [P, 2, DC, P], F32)
        hid = sb("hid", [P, 2, FC, P], F32)
        ys = sb("ys", [P, 2, D], F32)
        row_no = sb("row_no", [P, 2, 1], U32)

        consts_in = sem("consts_in")
        pad_set = sem("pad_set")
        zeroed = sem("zeroed")
        stats_done = sem("stats_done")
        xl_ready = sem("xl_ready")
        xn_ready = sem("xn_ready")
        xt_full = sem("xt_full")
        xt_copied = sem("xt_copied")
        logits_full = sem("logits_full")
        max_off = sem("max_off")
        exp_done = sem("exp_done")
        onehot_ready = sem("onehot_ready")
        ranks_full = sem("ranks_full")
        routed = sem("routed")
        scattered = sem("scattered")
        xs_in = [sem(f"xs_in{i}") for i in range(2)]
        w1_in = [sem(f"w1_in{i}") for i in range(2)]
        w2_in = [sem(f"w2_in{i}") for i in range(2)]
        h_full = sem("h_full")
        xst_full = sem("xst_full")
        xst_ready = sem("xst_ready")
        hid_ready = sem("hid_ready")
        y_full = sem("y_full")
        y_copied = sem("y_copied")
        y_stored = [sem(f"y_stored{i}") for i in range(2)]
        rows_known = sem("rows_known")
        waited = sem("waited")
        y_in = [sem(f"y_in{b}") for b in range(B)]
        dve_chain = sem("dve_chain")
        pool_step = sem("pool_step")
        numbered = sem("numbered")

        consts = ((rms_w, "rms_w"), (gate, "gate0"), (upper, "upper"), (tie, "tie"), (steps, "steps"), (before, "before"), (tile_no, "tile_no"), (number, "number"))
        w1_cols = DC * F
        n_tiles = SEL_TILES

        with nc.Block() as block:

            @block.sync
            def _(sp):
                for dst, src in consts:
                    sp.dma_start(dst[:], dram[src]).then_inc(consts_in, 16)
                sp.wait_ge(pad_set, 1)
                sp.dma_start(dram["xs"].rearrange("(n p) d -> p n d", p=P), pad[:]).then_inc(zeroed, 16)
                sp.wait_ge(routed, 1)
                xs_dram = dram["xs"].rearrange("(n p) d -> n p d", p=P)
                def turn_of_loop(i):
                    for k in range(2):
                        n = i * 2 + k
                        e = sp.value_load(expert[0:1, bass.ds(n, 1)], min_val=0, max_val=E - 1)
                        wait_from(sp, h_full, 2 * n - 2)
                        sp.dma_start(wts[:, k, 0:w1_cols], dram["w0"][bass.ds(e, 1), :, 0:w1_cols].rearrange("a p f -> (a p) f")).then_inc(w1_in[k], 16)
                        wait_from(sp, y_copied, n - 1)
                        sp.dma_start(wts[:, k, w1_cols:], dram["w0"][bass.ds(e, 1), :, w1_cols:].rearrange("a p f -> (a p) f")).then_inc(w2_in[k], 16)
                        if isinstance(n, int) and n == 0:
                            sp.wait_ge(scattered, 16 * NT)
                            sp.dma_start(xs[:, 0], xs_dram[0]).then_inc(xs_in[0], 16)
                        wait_from(sp, xst_full, n)
                        wait_from(sp, rows_known, n)
                        sp.dma_start(xs[:, 1 - k], xs_dram[bass.ds(n + 1, 1)].rearrange("a p d -> (a p) d")).then_inc(xs_in[1 - k], 16)

                turns(sp, n_tiles // 2, turn_of_loop)
                for k in range(2):
                    sp.wait_ge(y_stored[k], 16 * (n_tiles // 2))
                for b in range(B):
                    sp.dma_start(xn[:, TB * b:TB * (b + 1), 0:D], dram["ys"][T * b:T * (b + 1)].rearrange("(j p) d -> p j d", p=P)).then_inc(y_in[b], 16)

            @block.gpsimd
            def _(pool):
                pool.memset(pad[:], 0.0).then_inc(pool_step, 1)
                pool.wait_ge(pool_step, 1)
                pool.wait_ge(consts_in, 16 * len(consts))
                pool.tensor_copy(pad[:, :, D:ROW].bitcast(U32), number[:, NT:].unsqueeze(2)).then_inc(pad_set, 1)
                pool.tensor_copy(xn[:, :, D:ROW].bitcast(U32), number[:, 0:NT].unsqueeze(2)).then_inc(numbered, 1)
                pool.wait_ge(numbered, 1)
                pool.wait_ge(zeroed, 16)
                pool.wait_ge(routed, 1)
                for i in range(NT):
                    pool.indirect_dma_start(dram["xs"], bass.IndirectOffsetOnAxis(slot[:, i:i + 1], 0), xn[:, i], None).then_inc(scattered, 16)
                def turn_of_loop(it):
                    for k in range(2):
                        n = it * 2 + k
                        pool.wait_ge(xs_in[k], 16 * it + 16)
                        wait_from(pool, y_stored[k], 16 * it)
                        pool.sem_inc(waited, 1)
                        pool.tensor_copy(row_no[:, k], xs[:, k, D:ROW].bitcast(U32)).then_inc(rows_known, 1)
                        pool.wait_ge(y_copied, n + 1)
                        pool.wait_ge(rows_known, n + 1)
                        pool.sem_inc(waited, 1)
                        pool.indirect_dma_start(dram["ys"], bass.IndirectOffsetOnAxis(row_no[:, k], 0), ys[:, k], None).then_inc(y_stored[k], 16)

                turns(pool, n_tiles // 2, turn_of_loop)

            @block.scalar
            def _(act):
                for i in range(NT):
                    act.wait_ge(stats_done, 1)
                    nc.scalar.activation(xn[:, i, 0:D], x[:, i], ACT.Identity, bias=neg_mean[:, i:i + 1], scale=rstd[:, i:i + 1]).then_inc(xl_ready, 1)
                act.wait_ge(max_off, 1)
                nc.scalar.activation(prob[:], work[:], ACT.Exp).then_inc(exp_done, 1)
                def turn_of_loop(it):
                    for k in range(2):
                        n = it * 2 + k
                        act.wait_ge(w2_in[k], 16 * it + 16)
                        wait_from(act, y_full, n - 1)
                        for half in range(2):
                            act.wait_ge(h_full, 2 * n + half + 1)
                            for q in range(4):
                                fc = 4 * half + q
                                nc.scalar.activation(hid[:, k, fc], m.ps_st[:, 2 * k + half, q * P:(q + 1) * P], ACT.Silu,
                                                     bias=wts[:, k, w1_cols + FC * D + fc:w1_cols + FC * D + fc + 1]).then_inc(hid_ready, 1)

                turns(act, n_tiles // 2, turn_of_loop)
            @block.tensor
            def _(pe):
                for r in range(NT // 2 + 1):
                    if r < NT // 2:
                        pe.wait_ge(xn_ready, 2 * r + 2)
                        if r >= 2:
                            pe.wait_ge(xt_copied, r - 1)
                        for j in range(2):
                            for c in range(DC):
                                ins = pe.transpose(m.ps_max[:, r % 2, j * D + c * P:j * D + (c + 1) * P], xn[:, 2 * r + j, c * P:(c + 1) * P], m.ident[:])
                        ins.then_inc(xt_full, 1)
                    if r == 0:
                        pe.wait_ge(consts_in, 16 * len(consts))
                        continue
                    pe.wait_ge(xt_copied, r)
                    for j in range(2):
                        i = 2 * r - 2 + j
                        for c in range(DC):
                            ins = pe.matmul(m.ps_out[:, i * E:(i + 1) * E], xnt[:, (r - 1) % 2, j, c], gate[:, c], start=(c == 0), stop=(c == DC - 1))
                    ins.then_inc(logits_full, 1)
                pe.wait_ge(onehot_ready, 1)
                flat = onehot_b[:].rearrange("p n e -> p (n e)")
                for i in range(NT - 1):
                    pe.matmul(m.ps_misc[:, (i + 1) * E:NT * E].rearrange("p (n e) -> p n e", e=E), ones_b[:],
                              onehot_b[:, i:i + 1].to_broadcast([P, NT - 1 - i, E]), start=(i == 0), stop=False, skip_group_check=True)
                pe.matmul(m.ps_misc[:, 0:NT * E], upper_b[:], flat, start=False, stop=True, skip_group_check=True)
                for i in range(NT):
                    ins = pe.matmul(m.ps_max[:, 0, 0:E], ones_b[:], onehot_b[:, i], start=(i == 0), stop=(i == NT - 1))
                ins.then_inc(ranks_full, 1)

                def turn(k):
                    for c in range(DC):
                        ins = pe.transpose(m.ps_misc[:, c * P:(c + 1) * P], xs[:, k, c * P:(c + 1) * P], m.ident[:])
                    return ins

                pe.wait_ge(xs_in[0], 16)
                ins = turn(0)
                ins.then_inc(xst_full, 1)
                def turn_of_loop(it):
                    for k in range(2):
                        n = it * 2 + k
                        pe.wait_ge(w1_in[k], 16 * it + 16)
                        pe.wait_ge(xst_ready, n + 1)
                        for half in range(2):
                            wait_from(pe, hid_ready, 8 * n - 12 + 4 * half)
                            for q in range(4):
                                fc = 4 * half + q
                                for c in range(DC):
                                    ins = pe.matmul(m.ps_st[:, 2 * k + half, q * P:(q + 1) * P], wts[:, k, c * F + fc * P:c * F + (fc + 1) * P], xst[:, k, c],
                                                    start=(c == 0), stop=(c == DC - 1))
                            ins.then_inc(h_full, 1)
                        pe.wait_ge(xs_in[1 - k], (16 * it + 16) if k == 0 else (16 * it + 32))
                        turn(1 - k).then_inc(xst_full, 1)
                        pe.wait_ge(w2_in[k], 16 * it + 16)
                        wait_from(pe, y_copied, n - 1)
                        for fc in range(FC):
                            if fc % 4 == 0:
                                pe.wait_ge(hid_ready, 8 * n + 4 + fc)
                            ins = pe.matmul(m.ps_max[:, k, 0:D], hid[:, k, fc], wts[:, k, w1_cols + fc * D:w1_cols + (fc + 1) * D], start=(fc == 0), stop=(fc == FC - 1))
                        ins.then_inc(y_full, 1)

                turns(pe, n_tiles // 2, turn_of_loop)
            @block.vector
            def _(dve):
                chain = Counter(dve, dve_chain)
                dve.memset(ones_b[:], 1.0)
                for i in range(NT):
                    ins = dve.bn_stats(stats[:, i], x[:, i])
                chain.link(ins)
                for i in range(NT):
                    ins = dve.bn_aggr(mv[:, i], stats[:, i])
                chain.link(ins)
                rsqrt(dve, chain, rstd[:], mv[:, :, 1], [z[:] for z in tmp], 1.0 + RMS_EPS, LN_EPS * RMS_EPS)
                dve.scalar_tensor_tensor(neg_mean[:], mv[:, :, 0], -1.0, rstd[:], ALU.mult, ALU.mult).then_inc(stats_done, 1)
                dve.wait_ge(consts_in, 16 * len(consts))
                dve.tensor_copy(upper_b[:], upper[:])

                def copy_turned(r):
                    dve.wait_ge(xt_full, r + 1)
                    if r >= 2:
                        dve.wait_ge(logits_full, r - 1)
                    dve.tensor_copy(xnt[:, r % 2], m.ps_max[:, r % 2].rearrange("p (j c t) -> p j c t", j=2, c=DC)).then_inc(xt_copied, 1)

                for r in range(NT // 2):
                    for i in (2 * r, 2 * r + 1):
                        dve.wait_ge(xl_ready, i + 1)
                        dve.tensor_tensor(xn[:, i, 0:D], xn[:, i, 0:D], rms_w[:], ALU.mult).then_inc(xn_ready, 1)
                    if r:
                        copy_turned(r - 1)
                copy_turned(NT // 2 - 1)
                dve.wait_ge(logits_full, NT // 2)
                lg = m.ps_out[:, 0:NT * E].rearrange("p (n e) -> p n e", e=E)
                chain.link(dve.tensor_copy(logits[:], lg))
                chain.link(dve.tensor_reduce(top[:], logits[:], AX.X, ALU.max))
                dve.tensor_tensor(work[:], logits[:], top[:].unsqueeze(2).to_broadcast([P, NT, E]), ALU.subtract).then_inc(max_off, 1)
                dve.wait_ge(exp_done, 1)
                chain.link(dve.tensor_reduce(score[:], prob[:], AX.X, ALU.add))
                chain.link(dve.reciprocal(score[:], score[:]))
                chain.link(dve.tensor_tensor(prob[:], prob[:], score[:].unsqueeze(2).to_broadcast([P, NT, E]), ALU.mult))
                chain.link(dve.tensor_reduce(score[:], prob[:], AX.X, ALU.max))
                chain.link(dve.tensor_tensor(work[:], prob[:], score[:].unsqueeze(2).to_broadcast([P, NT, E]), ALU.is_ge))
                chain.link(dve.tensor_tensor(work[:], work[:], tie[:].unsqueeze(1).to_broadcast([P, NT, E]), ALU.mult))
                chain.link(dve.tensor_reduce(top[:], work[:], AX.X, ALU.max))
                chain.link(dve.tensor_tensor(onehot[:], work[:], top[:].unsqueeze(2).to_broadcast([P, NT, E]), ALU.is_equal))
                dve.tensor_copy(onehot_b[:], onehot[:]).then_inc(onehot_ready, 1)
                dve.wait_ge(ranks_full, 1)
                chain.link(dve.tensor_copy(count[:], m.ps_max[:, 0, 0:E]))
                chain.link(dve.tensor_tensor(cmp[:], count[:].unsqueeze(2).to_broadcast([P, E, NT]), steps[:].unsqueeze(1).to_broadcast([P, E, NT]), ALU.is_gt))
                chain.link(dve.tensor_reduce(tiles_e[:], cmp[:], AX.X, ALU.add))
                chain.link(dve.tensor_tensor(pre[:], before[:], tiles_e[:].unsqueeze(1).to_broadcast([P, E, E]), ALU.mult))
                chain.link(dve.tensor_reduce(base[:], pre[:], AX.X, ALU.add))
                chain.link(dve.tensor_tensor(last[:], base[:], tiles_e[:], ALU.add))
                chain.link(dve.tensor_scalar(base[:], base[:], float(P), None, ALU.mult))
                rank = m.ps_misc[:, 0:NT * E].rearrange("p (n e) -> p n e", e=E)
                chain.link(dve.tensor_tensor(work[:], rank, base[:].unsqueeze(1).to_broadcast([P, NT, E]), ALU.add))
                chain.link(dve.tensor_tensor(work[:], work[:], onehot[:], ALU.mult))
                chain.link(dve.tensor_reduce(slot_f[:], work[:], AX.X, ALU.add))
                chain.link(dve.tensor_copy(slot[:], slot_f[:]))
                chain.link(dve.tensor_tensor(which[:], last[:].unsqueeze(1).to_broadcast([P, SEL_TILES, E]), tile_no[:].unsqueeze(2).to_broadcast([P, SEL_TILES, E]), ALU.is_le))
                chain.link(dve.tensor_reduce(expert_f[:], which[:], AX.X, ALU.add))
                chain.link(dve.tensor_scalar(expert[:], expert_f[:], float(E - 1), None, ALU.min))
                dve.engine_nop().then_inc(routed, 1)
                dve.wait_ge(xst_full, 1)
                dve.tensor_copy(xst[:, 0], m.ps_misc[:, 0:D].rearrange("p (c t) -> p c t", c=DC)).then_inc(xst_ready, 1)
                def turn_of_loop(it):
                    for k in range(2):
                        n = it * 2 + k
                        dve.wait_ge(xst_full, n + 2)
                        dve.tensor_copy(xst[:, 1 - k], m.ps_misc[:, 0:D].rearrange("p (c t) -> p c t", c=DC)).then_inc(xst_ready, 1)
                        dve.wait_ge(y_full, n + 1)
                        wait_from(dve, y_stored[k], 16 * it)
                        dve.tensor_tensor(ys[:, k], m.ps_max[:, k, 0:D], wts[:, k, W0_COLS - D:W0_COLS], ALU.add).then_inc(y_copied, 1)

                turns(dve, n_tiles // 2, turn_of_loop)
                for i in range(NT):
                    dve.wait_ge(y_in[i // TB], 16)
                    dve.scalar_tensor_tensor(x[:, i], xn[:, i, 0:D], score[:, i:i + 1], x[:, i], ALU.mult, ALU.add)


def moe_top_k(nc, m, dram):
    with ExitStack() as ctx:
        def sb(name, shape, dt):
            return ctx.enter_context(nc.sbuf_tensor(f"e1_{name}", shape, dt))

        def sem(name):
            return m.ctx.enter_context(nc.semaphore(f"e1_{name}"))

        x = m.x
        NE = B * E
        xn = sb("xn", [P, NT, D], F32)
        xnt = sb("xnt", [P, 2, DC, P], F32)
        gate = sb("gate", [P, DC, E], F32)
        row_base = sb("row_base", [NE, 1], F32)
        zero = sb("zero", [P, D], F32)
        stats = sb("stats", [P, NT, 6], F32)
        mv = sb("mv", [P, NT, 2], F32)
        rstd = sb("rstd", [P, NT], F32)
        tmp = [sb(f"tmp{i}", [P, NT], F32) for i in range(2)]
        work = sb("work", [P, NT, E], F32)
        prob = sb("prob", [P, NT, E], F32)
        top = sb("top", [P, NT], F32)
        prob_j = sb("prob_j", [P, TB, B, E], F32)
        rows = sb("rows", [NE, 2, T], F32)
        best = sb("best", [NE, CAP], F32)
        best_at = sb("best_at", [NE, CAP], U32)
        best_tok = sb("best_tok", [NE, CAP], F32)
        gate_w = sb("gate_w", [P, B, E], F32)
        token = sb("token", [P, E + 1, B], U32)
        token_e = sb("token_e", [P, 2, B], U32)
        token_s = sb("token_s", [P, 2, B], U32)
        xg = sb("xg", [P, 2, B, D], F32)
        xt = sb("xt", [P, 2, DC, B * CAP], F32R)
        wf = sb("wf", [P, 2 * DC * F], F32)
        wr = sb("wr", [P, 2, 2 * DC * F], F32R)
        hf = sb("hf", [P, 2, B * CAP], F32)
        hr = sb("hr", [P, 2, FC, B * CAP], F32R)
        ys = sb("ys", [P, 2, B, D], F32)
        half_b = sb("half_b", [P, 2, TB, D], BF16)

        consts_in = sem("consts_in")
        zero_set = sem("zero_set")
        zeroed = sem("zeroed")
        xn_ready = sem("xn_ready")
        xn_stored = sem("xn_stored")
        xt_full = sem("xt_full")
        xt_copied = sem("xt_copied")
        logits_full = sem("logits_full")
        max_off = sem("max_off")
        exp_done = sem("exp_done")
        prob_ready = sem("prob_ready")
        rows_full = sem("rows_full")
        picked = sem("picked")
        picks_full = sem("picks_full")
        routed = sem("routed")
        token_ready = sem("token_ready")
        gathered = [sem(f"gathered{i}") for i in range(2)]
        w_in = [sem(f"w_in{i}") for i in range(2)]
        w_hi = [sem(f"w_hi{i}") for i in range(2)]
        w_lo = [sem(f"w_lo{i}") for i in range(2)]
        x_hi = sem("x_hi")
        h_hi = sem("h_hi")
        scatter_ready = sem("scatter_ready")
        waited = sem("waited")
        x_full = sem("x_full")
        x_split = sem("x_split")
        h_full = sem("h_full")
        h_copied = sem("h_copied")
        h_split = sem("h_split")
        y_full = sem("y_full")
        y_copied = sem("y_copied")
        y_added = [sem(f"y_added{i}") for i in range(2)]
        sum_in = sem("sum_in")
        out_ready = sem("out_ready")
        out_stored = sem("out_stored")
        dve_chain = sem("dve_chain")
        HALF = DC * F
        y_bank = (m.ps_out, m.ps_misc)

        with nc.Block() as block:

            @block.sync
            def _(sp):
                sp.dma_start(gate[:], dram["gate1"]).then_inc(consts_in, 16)
                sp.dma_start(row_base[:], dram["row_base"]).then_inc(consts_in, 16)
                sp.wait_ge(zero_set, 1)
                sp.dma_start(dram["acc"].rearrange("(n p) d -> p n d", p=P), zero[:].unsqueeze(1).to_broadcast([P, NT, D])).then_inc(zeroed, 16)
                for b in range(B):
                    sp.wait_ge(xn_ready, TB * (b + 1))
                    sp.dma_start(dram["xl"][b * T:(b + 1) * T].rearrange("(n p) d -> p n d", p=P), xn[:, TB * b:TB * (b + 1)]).then_inc(xn_stored, 16)
                def turn_of_loop(e):
                    for part in range(2):
                        wait_from(sp, w_lo[part], e)
                        sp.dma_start(wf[:, part * HALF:(part + 1) * HALF], dram["w1"][bass.ds(e, 1), :, part * HALF:(part + 1) * HALF].rearrange("a p f -> (a p) f")).then_inc(w_in[part], 16)

                turns(sp, E, turn_of_loop)
                for k in range(2):
                    sp.wait_ge(y_added[k], 16 * B * (E // 2))
                sp.dma_start(xn[:], dram["acc"].rearrange("(n p) d -> p n d", p=P)).then_inc(sum_in, 16)
                for b in range(B):
                    sp.wait_ge(out_ready, b + 1)
                    sp.dma_start(dram["out"][b].rearrange("(j p) d -> p j d", p=P), x[:, TB * b:TB * (b + 1)]).then_inc(out_stored, 16)
                sp.wait_ge(out_stored, 16 * B)

            @block.gpsimd
            def _(pool):
                pool.memset(zero[:], 0.0).then_inc(zero_set, 1)
                pool.wait_ge(routed, 1)
                pool.wait_ge(xn_stored, 16 * B)
                pool.wait_ge(zeroed, 16)

                def gather(e, k):
                    pool.tensor_copy(token_e[:, k].unsqueeze(1), token[:, bass.ds(e, 1)]).then_inc(token_ready, 1)
                    pool.wait_ge(token_ready, e + 1)
                    pool.sem_inc(waited, 1)
                    for b in range(B):
                        pool.indirect_dma_start(xg[:, k, b], None, dram["xl"], bass.IndirectOffsetOnAxis(token_e[:, k, b:b + 1], 0)).then_inc(gathered[k], 16)

                def scatter(e, it, k):
                    pool.wait_ge(y_copied, B * e + B)
                    wait_from(pool, y_added[1 - k], 16 * B * (it + k))
                    pool.sem_inc(waited, 1)
                    for b in range(B):
                        pool.indirect_dma_start(dram["acc"], bass.IndirectOffsetOnAxis(token_s[:, k, b:b + 1], 0), ys[:, k, b], None,
                                                compute_op=ALU.add).then_inc(y_added[k], 16)

                def low_part(part, e):
                    pool.wait_ge(w_hi[part], e + 1)
                    cols = slice(part * HALF, (part + 1) * HALF)
                    pool.tensor_tensor(wr[:, 1, cols], wf[:, cols], wr[:, 0, cols].bitcast(F32), ALU.subtract).then_inc(w_lo[part], 1)

                def turn_of_loop(it):
                    for k in range(2):
                        e = it * 2 + k
                        low_part(0, e)
                        wait_from(pool, x_full, e)
                        gather(e + 1, 1 - k)
                        low_part(1, e)
                        if not isinstance(e, int) or e > 0:
                            pool.tensor_copy(token_s[:, 1 - k].unsqueeze(1), token[:, bass.ds(e - 1, 1)]).then_inc(scatter_ready, 1)
                            pool.wait_ge(scatter_ready, e)
                            scatter(e - 1, it + k - 1, 1 - k)

                gather(0, 0)
                turns(pool, E // 2, turn_of_loop)
                pool.tensor_copy(token_s[:, 1].unsqueeze(1), token[:, E - 1:E]).then_inc(scatter_ready, 1)
                pool.wait_ge(scatter_ready, E)
                scatter(E - 1, E // 2 - 1, 1)

            @block.scalar
            def _(act):
                for i in range(NT):
                    act.wait_ge(xt_full, i + 1)
                    if i >= 2:
                        act.wait_ge(logits_full, i - 1)
                    nc.scalar.copy(xnt[:, i % 2], m.ps_max[:, i % 2, 0:D].rearrange("p (c t) -> p c t", c=DC)).then_inc(xt_copied, 1)
                act.wait_ge(max_off, 1)
                nc.scalar.activation(prob[:], work[:], ACT.Exp).then_inc(exp_done, 1)
                def turn_of_loop(e):
                    for part, (used, n) in enumerate(((h_full, FC), (y_full, B))):
                        act.wait_ge(w_in[part], 16 * e + 16)
                        wait_from(act, used, n * e)
                        cols = slice(part * HALF, (part + 1) * HALF)
                        nc.scalar.copy(wr[:, 0, cols], wf[:, cols]).then_inc(w_hi[part], 1)
                    for fc in range(FC):
                        act.wait_ge(h_full, FC * e + fc + 1)
                        wait_from(act, h_split, FC * e + fc - 1)
                        nc.scalar.activation(hf[:, fc % 2], m.ps_st[:, fc % 4], ACT.Gelu_apprx_tanh).then_inc(h_copied, 1)

                turns(act, E, turn_of_loop)
            @block.tensor
            def _(pe):
                for i in range(NT + 1):
                    if i < NT:
                        pe.wait_ge(xn_ready, i + 1)
                        if i >= 2:
                            pe.wait_ge(xt_copied, i - 1)
                        for c in range(DC):
                            ins = pe.transpose(m.ps_max[:, i % 2, c * P:(c + 1) * P], xn[:, i, c * P:(c + 1) * P], m.ident[:])
                        ins.then_inc(xt_full, 1)
                    if i == 0:
                        pe.wait_ge(consts_in, 32)
                        continue
                    pe.wait_ge(xt_copied, i)
                    for c in range(DC):
                        ins = pe.matmul(m.ps_out[:, (i - 1) * E:i * E], xnt[:, (i - 1) % 2, c], gate[:, c], start=(c == 0), stop=(c == DC - 1))
                    ins.then_inc(logits_full, 1)
                pe.wait_ge(prob_ready, 1)
                for j in range(TB):
                    ins = pe.transpose(m.ps_misc[0:NE, j * P:(j + 1) * P], prob_j[:, j].rearrange("p b e -> p (b e)"), m.ident[:])
                ins.then_inc(rows_full, 1)
                pe.wait_ge(picked, 1)
                pe.transpose(m.ps_misc[:, 0:NE], best_tok[:], m.ident[0:NE, 0:NE])
                pe.transpose(m.ps_misc[:, NE:2 * NE], best[:], m.ident[0:NE, 0:NE]).then_inc(picks_full, 1)

                def turn(k):
                    for c in range(DC):
                        for b in range(B):
                            ins = pe.transpose(m.ps_max[:, c, b * P:(b + 1) * P], xg[:, k, b, c * P:(c + 1) * P], m.ident[:])
                    ins.then_inc(x_full, 1)

                pe.wait_ge(gathered[0], 16 * B)
                turn(0)
                terms = ((0, 0), (1, 0), (0, 1))
                def turn_of_loop(it):
                    for k in range(2):
                        e = it * 2 + k
                        pe.wait_ge(w_lo[0], e + 1)
                        pe.wait_ge(x_split, e + 1)
                        for fc in range(FC):
                            wait_from(pe, h_copied, FC * e + fc - 3)
                            for c in range(DC):
                                for wp, xp in terms:
                                    ins = pe.matmul(m.ps_st[:, fc % 4], wr[:, wp, c * F + fc * P:c * F + (fc + 1) * P], xt[:, xp, c],
                                                    start=(c == 0 and (wp, xp) == (0, 0)), stop=(c == DC - 1 and (wp, xp) == (0, 1)))
                            ins.then_inc(h_full, 1)
                        pe.wait_ge(gathered[1 - k], (16 * B * it + 16 * B) if k == 0 else (16 * B * it + 32 * B))
                        turn(1 - k)
                        pe.wait_ge(w_lo[1], e + 1)
                        for b in range(B):
                            wait_from(pe, y_copied, B * e + b - 1)
                            for fc in range(FC):
                                if b == 0:
                                    pe.wait_ge(h_split, FC * e + fc + 1)
                                for hp, wp in terms:
                                    ins = pe.matmul(y_bank[b % 2][:, 0:D], hr[:, hp, fc, b * P:(b + 1) * P], wr[:, wp, HALF + fc * D:HALF + (fc + 1) * D],
                                                    start=(fc == 0 and (hp, wp) == (0, 0)), stop=(fc == FC - 1 and (hp, wp) == (0, 1)))
                            ins.then_inc(y_full, 1)

                turns(pe, E // 2, turn_of_loop)
            @block.vector
            def _(dve):
                chain = Counter(dve, dve_chain)
                for i in range(NT):
                    ins = dve.bn_stats(stats[:, i], x[:, i])
                chain.link(ins)
                for i in range(NT):
                    ins = dve.bn_aggr(mv[:, i], stats[:, i])
                chain.link(ins)
                rsqrt(dve, chain, rstd[:], mv[:, :, 1], [z[:] for z in tmp], 1.0, LN_EPS)
                for i in range(NT):
                    dve.tensor_scalar(xn[:, i], x[:, i], mv[:, i, 0:1], rstd[:, i:i + 1], ALU.subtract, ALU.mult).then_inc(xn_ready, 1)
                dve.wait_ge(logits_full, NT)
                lg = m.ps_out[:, 0:NT * E].rearrange("p (n e) -> p n e", e=E)
                chain.link(dve.tensor_reduce(top[:], lg, AX.X, ALU.max))
                dve.tensor_tensor(work[:], lg, top[:].unsqueeze(2).to_broadcast([P, NT, E]), ALU.subtract).then_inc(max_off, 1)
                dve.wait_ge(exp_done, 1)
                chain.link(dve.tensor_reduce(top[:], prob[:], AX.X, ALU.add))
                chain.link(dve.reciprocal(top[:], top[:]))
                dve.tensor_tensor(prob_j[:].rearrange("p j b e -> p b j e"), prob[:].rearrange("p (b j) e -> p b j e", b=B),
                                  top[:].rearrange("p (b j) -> p b j", b=B).unsqueeze(3).to_broadcast([P, B, TB, E]), ALU.mult).then_inc(prob_ready, 1)
                dve.wait_ge(rows_full, 1)
                chain.link(dve.tensor_copy(rows[:, 0], m.ps_misc[0:NE]))
                for r in range(CAP // 8):
                    cols = slice(8 * r, 8 * r + 8)
                    chain.link(dve.max(best[:, cols], rows[:, r % 2]))
                    chain.link(dve.max_index(best_at[:, cols], best[:, cols], rows[:, r % 2]))
                    if r < CAP // 8 - 1:
                        chain.link(dve.match_replace(rows[:, (r + 1) % 2], best[:, cols], rows[:, r % 2], -1.0))
                dve.wait_ge(consts_in, 32)
                dve.tensor_scalar(best_tok[:], best_at[:], row_base[:], None, ALU.add).then_inc(picked, 1)
                dve.wait_ge(picks_full, 1)
                chain.link(dve.tensor_copy(token[:, 0:E].rearrange("p e b -> p b e"), m.ps_misc[:, 0:NE].rearrange("p (b e) -> p b e", e=E)))
                dve.tensor_copy(token[:, E], token[:, 0])
                chain.link(dve.tensor_copy(gate_w[:], m.ps_misc[:, NE:2 * NE].rearrange("p (b e) -> p b e", e=E)))
                dve.engine_nop().then_inc(routed, 1)

                def split_x(e):
                    dve.wait_ge(x_full, e + 1)
                    dve.tensor_copy(xt[:, 0], m.ps_max[:]).then_inc(x_hi, 1)
                    dve.wait_ge(x_hi, e + 1)
                    dve.tensor_tensor(xt[:, 1], m.ps_max[:], xt[:, 0].bitcast(F32), ALU.subtract).then_inc(x_split, 1)

                split_x(0)
                def turn_of_loop(it):
                    for k in range(2):
                        e = it * 2 + k
                        for fc in range(FC):
                            dve.wait_ge(h_copied, FC * e + fc + 1)
                            dve.tensor_copy(hr[:, 0, fc], hf[:, fc % 2]).then_inc(h_hi, 1)
                            dve.wait_ge(h_hi, FC * e + fc + 1)
                            dve.tensor_tensor(hr[:, 1, fc], hf[:, fc % 2], hr[:, 0, fc].bitcast(F32), ALU.subtract).then_inc(h_split, 1)
                        split_x(e + 1)
                        wait_from(dve, y_added[k], 16 * B * it)
                        for b in range(B):
                            dve.wait_ge(y_full, B * e + b + 1)
                            dve.tensor_scalar(ys[:, k, b], y_bank[b % 2][:, 0:D], gate_w[:, b, bass.ds(e, 1)], None, ALU.mult).then_inc(y_copied, 1)

                turns(dve, E // 2, turn_of_loop)
                dve.wait_ge(sum_in, 16)
                for b in range(B):
                    if b >= 2:
                        dve.wait_ge(out_ready, b - 1)
                    chain.link(dve.tensor_copy(half_b[:, b % 2], xn[:, TB * b:TB * (b + 1)]))
                    dve.tensor_tensor(x[:, TB * b:TB * (b + 1)], x[:, TB * b:TB * (b + 1)], half_b[:, b % 2], ALU.add).then_inc(out_ready, 1)


def setup(nc, ctx, dram):
    m = Memory()
    m.ctx = ctx
    m.x = ctx.enter_context(nc.sbuf_tensor("x_res", [P, NT, D], F32))
    m.ident = ctx.enter_context(nc.sbuf_tensor("ident", [P, P], F32))
    m.ps_max = ctx.enter_context(nc.psum_tensor("ps_max", [P, 2, 512], F32))
    m.ps_st = ctx.enter_context(nc.psum_tensor("ps_st", [P, 4, 512], F32))
    m.ps_out = ctx.enter_context(nc.psum_tensor("ps_out", [P, 512], F32))
    m.ps_misc = ctx.enter_context(nc.psum_tensor("ps_misc", [P, 512], F32))
    m.ident_in = ctx.enter_context(nc.semaphore("ident_in"))
    for name, shape in (("q_scr", (B, 2, D, T)), ("k_scr", (B, 2, D, T)), ("xs", ((SEL_TILES + 1) * P, ROW)),
                        ("ys", (B * T + (SEL_TILES + 1) * P, D)), ("xl", (B * T, D)), ("acc", (B * T, D))):
        dram[name] = nc.dram_tensor(f"scratch_{name}", shape, F32).ap()
    return m, (lambda: attention(nc, m, 0, dram), lambda: moe_top1(nc, m, dram),
               lambda: attention(nc, m, 1, dram), lambda: moe_top_k(nc, m, dram))


def program(nc, dram):
    with ExitStack() as ctx:
        _, stages = setup(nc, ctx, dram)
        for stage in stages:
            stage()


def shape_constants(np):
    f = np.float32
    inv = (f(1.0) / (f(10000.0) ** (np.arange(0, HD, 2, dtype=f) / f(HD)))).astype(f)
    angle = np.outer(np.arange(T, dtype=f), inv).astype(f)
    angle = np.concatenate([angle, angle], axis=-1)
    cos, sin = np.cos(angle).astype(f), np.sin(angle).astype(f)
    sin[:, :HD // 2] *= -1
    per_q = lambda a: np.ascontiguousarray((a * f(HD ** -0.5)).reshape(TB, P, HD).transpose(1, 0, 2))

    def parts(a):
        bits = a.view(np.uint32)
        hi = ((bits + np.uint32(0x800)) & np.uint32(0xFFFFF000)).view(f)
        return hi, (a - hi).astype(f)

    slopes = np.array([2.0 ** (-8.0 * i / H) for i in range(1, H + 1)], dtype=f)
    bias = (slopes[:, None] * np.arange(T, dtype=f)[None]).reshape(NG, HG, T).astype(f)
    one = np.ones_like(bias)
    k_bias = np.stack([*parts(bias), one, one])
    q_bias = np.stack([one, one, *parts(-bias)])
    k_select = np.zeros((2, HG, NG, HG, T), f)
    for h in range(HG):
        k_select[:, h, :, h] = 1
    e = np.arange(E)
    full = lambda a: np.ascontiguousarray(np.broadcast_to(a, (P, *a.shape)).astype(f))
    return {
        "cos_t": np.ascontiguousarray(np.tile(cos.T, (P // HD, 1))), "sin_t": np.ascontiguousarray(np.tile(sin.T, (P // HD, 1))),
        "cos_q": per_q(cos), "sin_q": per_q(sin),
        "ident": np.eye(P, dtype=f),
        "k_bias": k_bias, "q_bias": q_bias, "k_select": k_select.reshape(MAX_ROWS, NG, HG, T),
        "upper": np.triu(np.ones((P, P), f), 1),
        "tie": full(f(E) - e.astype(f)),
        "steps": full(P * np.arange(NT, dtype=f)),
        "before": full((e[None] < e[:, None]).astype(f)),
        "number": (np.arange(NT + SEL_TILES + 1)[None] * P + np.arange(P)[:, None]).astype(np.uint32),
        "tile_no": full(np.arange(SEL_TILES, dtype=f)),
        "row_base": (np.arange(B * E) // E * T).astype(f)[:, None],
    }


def laid_out(np, i):
    chunks = lambda w: np.ascontiguousarray(w.reshape(DC, P, -1).transpose(1, 0, 2))
    ctx = np.asarray(i["ctx_1024"])
    ctx_t = np.ascontiguousarray(ctx.transpose(0, 2, 1))
    swap = np.arange(D).reshape(H, 2, HD // 2)[:, ::-1].reshape(D)
    rep = lambda v: np.ascontiguousarray(np.broadcast_to(v, (P, v.shape[-1])))

    def experts(w1, w2):
        return (w1.reshape(E, DC, P, F).transpose(0, 2, 1, 3).reshape(E, P, DC * F),
                w2.reshape(E, FC, P, D).transpose(0, 2, 1, 3).reshape(E, P, FC * D))

    a1, a2 = experts(np.asarray(i["L0_ffn_W1"]), np.asarray(i["L0_ffn_W2"]))
    b1 = np.asarray(i["L0_ffn_b1"]).reshape(E, FC, P).transpose(0, 2, 1)
    b2 = np.broadcast_to(np.asarray(i["L0_ffn_b2"])[:, None], (E, P, D))
    return {
        "x": np.asarray(i["x"]), "ctx": ctx, "ctx_t": ctx_t, "ctx_r": np.ascontiguousarray(ctx_t[:, swap]),
        "rms_w": rep(np.asarray(i["L0_ffn_rms_w"])),
        "gate0": chunks(np.asarray(i["L0_ffn_gate_w"]).T),
        "w0": np.ascontiguousarray(np.concatenate([a1, a2, b1, b2], axis=2)),
        "wq": chunks(np.asarray(i["L1_xattn_Wq"]).T), "wk": chunks(np.asarray(i["L1_xattn_Wk"]).T),
        "wv": chunks(np.asarray(i["L1_xattn_Wv"]).T), "wo": chunks(np.asarray(i["L1_xattn_Wo"]).T),
        "bqk": np.ascontiguousarray(np.stack([np.asarray(i["L1_xattn_bq"]).reshape(DC, P).T, np.asarray(i["L1_xattn_bk"]).reshape(DC, P).T], axis=1)),
        "bv": rep(np.asarray(i["L1_xattn_bv"])), "bo": rep(np.asarray(i["L1_xattn_bo"])),
        "gate1": chunks(np.asarray(i["L1_ffn_gate_w"])),
        "w1": np.ascontiguousarray(np.concatenate(experts(np.asarray(i["L1_ffn_w1"]), np.asarray(i["L1_ffn_w2"])), axis=2)),
    }


def kernel(**inputs):
    import numpy as np
    import concourse.bacc as bacc
    from concourse import mybir as _mybir
    from concourse.bass_utils import run_bass_kernel_spmd as run

    nc = bacc.Bacc("TRN2", target_bir_lowering=False, num_devices=1)
    arrays, dram = {}, {}
    for name, a in {**laid_out(np, inputs), **shape_constants(np)}.items():
        arrays[f"in_{name}"] = a
        dram[name] = nc.dram_tensor(f"in_{name}", a.shape, _mybir.dt.from_np(a.dtype), kind="ExternalInput").ap()
    dram["out"] = nc.dram_tensor("out_x", (B, T, D), F32, kind="ExternalOutput").ap()
    program(nc, dram)
    return run(nc, [arrays], core_ids=[0]).results[0]["out_x"]
```
